# Optimizing a Trainium2 kernel written in Bass

```python
import numpy as np
import jax
import jax.numpy as jnp

def _softmax(x, axis=-1):
    return jax.nn.softmax(x, axis=axis)

def _gelu(x):
    return jax.nn.gelu(x, approximate=True)

def _silu(x):
    return jax.nn.silu(x)

def _sigmoid(x):
    return jax.nn.sigmoid(x)

def _layernorm(x, axis=-1, eps=1e-05):
    m = jnp.mean(x, axis=axis, keepdims=True)
    v = jnp.var(x, axis=axis, keepdims=True)
    return (x - m) / jnp.sqrt(v + eps)

def _scatter_add(tgt, idx, src, axis=0):
    return tgt.at[idx].add(src)

def _segment_sum(src, seg, n):
    return jax.ops.segment_sum(src, seg, n)
kernel_name = 'mk_hybrid_d1_jaxref_r8_86414c'

def setup_inputs(seed: int=0):
    np.random.seed(seed)
    _w = jnp.asarray

    def _L0_attn_a_setup():
        import jax, jax.numpy as jnp
        import numpy as np
        D_MODEL = 256
        NUM_HEADS = 16
        HEAD_DIM = D_MODEL // NUM_HEADS
        SCALE = HEAD_DIM ** (-0.5)
        ALPHA = 1.0
        key = jax.random.key(seed)
        ks = jax.random.split(key, 9)
        B, T = (2, 256)
        s = 0.02
        w = lambda k: jax.random.normal(k, (D_MODEL, D_MODEL), jnp.float32) * s
        b = lambda k: jax.random.normal(k, (D_MODEL,), jnp.float32) * s
        return {'x': jax.random.normal(ks[0], (B, T, D_MODEL), jnp.float32), 'q_w': w(ks[1]), 'q_b': b(ks[2]), 'k_w': w(ks[3]), 'k_b': b(ks[4]), 'v_w': w(ks[5]), 'v_b': b(ks[6]), 'o_w': w(ks[7]), 'o_b': b(ks[8])}
    _L0_attn_a_in = _L0_attn_a_setup()

    def _L0_attn_b_setup():
        import jax, jax.numpy as jnp
        import numpy as np
        D_MODEL = 256
        HEADS = 16
        HEAD_DIM = D_MODEL // HEADS
        key = jax.random.key(seed)
        ks = jax.random.split(key, 9)
        s = 1.0 / np.sqrt(D_MODEL)
        return {'input_sequences': jax.random.normal(ks[0], (4, 256, D_MODEL), jnp.float32), 'Wq': jax.random.normal(ks[1], (D_MODEL, D_MODEL), jnp.float32) * s, 'bq': jax.random.normal(ks[2], (D_MODEL,), jnp.float32) * 0.01, 'Wk': jax.random.normal(ks[3], (D_MODEL, D_MODEL), jnp.float32) * s, 'bk': jax.random.normal(ks[4], (D_MODEL,), jnp.float32) * 0.01, 'Wv': jax.random.normal(ks[5], (D_MODEL, D_MODEL), jnp.float32) * s, 'bv': jax.random.normal(ks[6], (D_MODEL,), jnp.float32) * 0.01, 'Wo': jax.random.normal(ks[7], (D_MODEL, D_MODEL), jnp.float32) * s, 'bo': jax.random.normal(ks[8], (D_MODEL,), jnp.float32) * 0.01}
    _L0_attn_b_in = _L0_attn_b_setup()

    def _L0_ffn_setup():
        import jax, jax.numpy as jnp
        import numpy as np
        D_MODEL = 256
        D_HIDDEN = 176
        NUM_SHARED = 2
        NUM_ROUTED = 32
        TOP_K = 6

        def _expert_apply(xf, w1, b1, w2, b2):
            return jnp.maximum(xf @ w1 + b1, 0.0) @ w2 + b2
        key = jax.random.key(seed)
        ks = jax.random.split(key, 11)
        d, h = (D_MODEL, D_HIDDEN)
        s1 = 1.0 / np.sqrt(d)
        s2 = 1.0 / np.sqrt(h)
        x = jax.random.normal(ks[0], (2, 256, d), dtype=jnp.float32)
        sw1 = jax.random.uniform(ks[1], (NUM_SHARED, d, h), jnp.float32, -s1, s1)
        sb1 = jax.random.uniform(ks[2], (NUM_SHARED, h), jnp.float32, -s1, s1)
        sw2 = jax.random.uniform(ks[3], (NUM_SHARED, h, d), jnp.float32, -s2, s2)
        sb2 = jax.random.uniform(ks[4], (NUM_SHARED, d), jnp.float32, -s2, s2)
        rw1 = jax.random.uniform(ks[5], (NUM_ROUTED, d, h), jnp.float32, -s1, s1)
        rb1 = jax.random.uniform(ks[6], (NUM_ROUTED, h), jnp.float32, -s1, s1)
        rw2 = jax.random.uniform(ks[7], (NUM_ROUTED, h, d), jnp.float32, -s2, s2)
        rb2 = jax.random.uniform(ks[8], (NUM_ROUTED, d), jnp.float32, -s2, s2)
        router_w = jax.random.uniform(ks[9], (d, NUM_ROUTED), jnp.float32, -s1, s1)
        router_b = jax.random.uniform(ks[10], (NUM_ROUTED,), jnp.float32, -s1, s1)
        return {'x': x, 'sw1': sw1, 'sb1': sb1, 'sw2': sw2, 'sb2': sb2, 'rw1': rw1, 'rb1': rb1, 'rw2': rw2, 'rb2': rb2, 'router_w': router_w, 'router_b': router_b}
    _L0_ffn_in = _L0_ffn_setup()
    _d = {'L0_attn_a_x': _L0_attn_a_in['x'], 'L0_attn_a_q_w': _L0_attn_a_in['q_w'], 'L0_attn_a_q_b': _L0_attn_a_in['q_b'], 'L0_attn_a_k_w': _L0_attn_a_in['k_w'], 'L0_attn_a_k_b': _L0_attn_a_in['k_b'], 'L0_attn_a_v_w': _L0_attn_a_in['v_w'], 'L0_attn_a_v_b': _L0_attn_a_in['v_b'], 'L0_attn_a_o_w': _L0_attn_a_in['o_w'], 'L0_attn_a_o_b': _L0_attn_a_in['o_b'], 'L0_attn_b_Wq': _L0_attn_b_in['Wq'], 'L0_attn_b_bq': _L0_attn_b_in['bq'], 'L0_attn_b_Wk': _L0_attn_b_in['Wk'], 'L0_attn_b_bk': _L0_attn_b_in['bk'], 'L0_attn_b_Wv': _L0_attn_b_in['Wv'], 'L0_attn_b_bv': _L0_attn_b_in['bv'], 'L0_attn_b_Wo': _L0_attn_b_in['Wo'], 'L0_attn_b_bo': _L0_attn_b_in['bo'], 'L0_ffn_sw1': _L0_ffn_in['sw1'], 'L0_ffn_sb1': _L0_ffn_in['sb1'], 'L0_ffn_sw2': _L0_ffn_in['sw2'], 'L0_ffn_sb2': _L0_ffn_in['sb2'], 'L0_ffn_rw1': _L0_ffn_in['rw1'], 'L0_ffn_rb1': _L0_ffn_in['rb1'], 'L0_ffn_rw2': _L0_ffn_in['rw2'], 'L0_ffn_rb2': _L0_ffn_in['rb2'], 'L0_ffn_router_w': _L0_ffn_in['router_w'], 'L0_ffn_router_b': _L0_ffn_in['router_b']}
    _x0 = _d['L0_attn_a_x']
    _d['L0_attn_a_x'] = jax.random.normal(jax.random.fold_in(jax.random.key(seed), 1), (4, 1024, 256), dtype=_x0.dtype)
    del _x0
    return _d

def reference(L0_attn_a_x, L0_attn_a_q_w, L0_attn_a_q_b, L0_attn_a_k_w, L0_attn_a_k_b, L0_attn_a_v_w, L0_attn_a_v_b, L0_attn_a_o_w, L0_attn_a_o_b, L0_attn_b_Wq, L0_attn_b_bq, L0_attn_b_Wk, L0_attn_b_bk, L0_attn_b_Wv, L0_attn_b_bv, L0_attn_b_Wo, L0_attn_b_bo, L0_ffn_sw1, L0_ffn_sb1, L0_ffn_sw2, L0_ffn_sb2, L0_ffn_rw1, L0_ffn_rb1, L0_ffn_rw2, L0_ffn_rb2, L0_ffn_router_w, L0_ffn_router_b):

    def _L0_attn_a_ref(x, q_w, q_b, k_w, k_b, v_w, v_b, o_w, o_b):
        import jax, jax.numpy as jnp
        import numpy as np
        D_MODEL = 256
        NUM_HEADS = 16
        HEAD_DIM = D_MODEL // NUM_HEADS
        SCALE = HEAD_DIM ** (-0.5)
        ALPHA = 1.0
        B, T, D = x.shape
        H, HD = (NUM_HEADS, HEAD_DIM)

        def proj_split(w, bias):
            y = x @ w.T + bias
            return y.reshape(B, T, H, HD).transpose(0, 2, 1, 3).reshape(B * H, T, HD)
        Q = proj_split(q_w, q_b)
        K = proj_split(k_w, k_b)
        V = proj_split(v_w, v_b)
        S = jnp.einsum('hid,hjd->hij', K, Q) * SCALE
        idx = jnp.arange(T)
        delta = idx[:, None] - idx[None, :]
        decay = jnp.where(delta < 0, 0.0, -delta.astype(jnp.float32) ** ALPHA)
        S = jnp.where(delta < 0, -jnp.inf, S) + decay
        C = jax.nn.softmax(S, axis=-1)
        attn = jnp.einsum('hij,hjd->hid', C, V)
        attn = attn.reshape(B, H, T, HD).transpose(0, 2, 1, 3).reshape(B, T, D)
        return attn @ o_w.T + o_b

    def _L0_attn_b_ref(input_sequences, Wq, bq, Wk, bk, Wv, bv, Wo, bo):
        import jax, jax.numpy as jnp
        import numpy as np
        D_MODEL = 256
        HEADS = 16
        HEAD_DIM = D_MODEL // HEADS
        B, S, D = input_sequences.shape
        q = input_sequences @ Wq + bq
        k = input_sequences @ Wk + bk
        v = input_sequences @ Wv + bv
        q = q.reshape(B, S, HEADS, HEAD_DIM).transpose(0, 2, 1, 3)
        k = k.reshape(B, S, HEADS, HEAD_DIM).transpose(0, 2, 1, 3)
        v = v.reshape(B, S, HEADS, HEAD_DIM).transpose(0, 2, 1, 3)
        scores = jnp.einsum('bhqd,bhkd->bhqk', q, k) / np.sqrt(HEAD_DIM).astype(np.float32)
        causal = jnp.tril(jnp.ones((S, S), dtype=bool))
        scores = jnp.where(causal, scores, -jnp.inf)
        weights = jax.nn.softmax(scores, axis=-1)
        ctx = jnp.einsum('bhqk,bhkd->bhqd', weights, v)
        ctx = ctx.transpose(0, 2, 1, 3).reshape(B, S, D)
        return ctx @ Wo + bo

    def _L0_ffn_ref(x, sw1, sb1, sw2, sb2, rw1, rb1, rw2, rb2, router_w, router_b):
        import jax, jax.numpy as jnp
        import numpy as np
        D_MODEL = 256
        D_HIDDEN = 176
        NUM_SHARED = 2
        NUM_ROUTED = 32
        TOP_K = 6

        def _expert_apply(xf, w1, b1, w2, b2):
            return jnp.maximum(xf @ w1 + b1, 0.0) @ w2 + b2
        B, S, d = x.shape
        flat = x.reshape(-1, d)
        T = flat.shape[0]

        def sh_body(acc, p):
            w1, b1, w2, b2 = p
            return (acc + _expert_apply(flat, w1, b1, w2, b2), None)
        shared_out, _ = jax.lax.scan(sh_body, jnp.zeros_like(flat), (sw1, sb1, sw2, sb2))
        shared_out = shared_out / NUM_SHARED
        logits = flat @ router_w + router_b
        probs = jax.nn.softmax(logits, axis=-1)
        topk_p, topk_i = jax.lax.top_k(probs, TOP_K)
        topk_p = topk_p / jnp.sum(topk_p, axis=-1, keepdims=True)
        gates = jnp.zeros((T, NUM_ROUTED), dtype=flat.dtype)
        gates = gates.at[jnp.arange(T)[:, None], topk_i].add(topk_p)

        def r_body(acc, p):
            w1, b1, w2, b2, g = p
            return (acc + g[:, None] * _expert_apply(flat, w1, b1, w2, b2), None)
        routed_out, _ = jax.lax.scan(r_body, jnp.zeros_like(flat), (rw1, rb1, rw2, rb2, gates.T))
        return (shared_out + routed_out).reshape(B, S, d)
    x = L0_attn_a_x
    x = x + _L0_attn_a_ref(_layernorm(x, axis=-1), L0_attn_a_q_w, L0_attn_a_q_b, L0_attn_a_k_w, L0_attn_a_k_b, L0_attn_a_v_w, L0_attn_a_v_b, L0_attn_a_o_w, L0_attn_a_o_b)
    x = x + _L0_ffn_ref(_layernorm(x, axis=-1), L0_ffn_sw1, L0_ffn_sb1, L0_ffn_sw2, L0_ffn_sb2, L0_ffn_rw1, L0_ffn_rb1, L0_ffn_rw2, L0_ffn_rb2, L0_ffn_router_w, L0_ffn_router_b)
    x = x + _L0_attn_b_ref(_layernorm(x, axis=-1), L0_attn_b_Wq, L0_attn_b_bq, L0_attn_b_Wk, L0_attn_b_bk, L0_attn_b_Wv, L0_attn_b_bv, L0_attn_b_Wo, L0_attn_b_bo)
    x = x + _L0_ffn_ref(_layernorm(x, axis=-1), L0_ffn_sw1, L0_ffn_sb1, L0_ffn_sw2, L0_ffn_sb2, L0_ffn_rw1, L0_ffn_rb1, L0_ffn_rw2, L0_ffn_rb2, L0_ffn_router_w, L0_ffn_router_b)
    return x

_drawn_inputs = setup_inputs


def setup_inputs(seed=0):
    import zlib

    import numpy as np

    out = dict(_drawn_inputs(seed))
    spreads = {}
    factors = {'L0_attn_a_q_w': 6.829,
     'L0_attn_a_q_b': 64.0,
     'L0_attn_a_k_w': 6.67,
     'L0_attn_a_k_b': 32.486,
     'L0_attn_a_v_b': 4.581,
     'L0_attn_b_bq': 40.595,
     'L0_attn_b_bk': 64.0,
     'L0_attn_b_bv': 4.886,
     'L0_attn_b_bo': 5.038,
     'L0_ffn_rb1': 4.636}
    for name, (base, spread) in spreads.items():
        noise = np.random.default_rng([zlib.crc32(name.encode()), seed]).standard_normal(out[name].shape)
        drawn = base * np.exp(spread * noise) if base else spread * noise
        out[name] = jnp.asarray(drawn.astype(out[name].dtype))
    for name, factor in factors.items():
        out[name] = (out[name] * factor).astype(out[name].dtype)
    return out
```

```python
from contextlib import ExitStack

import numpy as np

import concourse.bass as bass
from concourse import mybir

F32 = mybir.dt.float32
F32R = mybir.dt.float32r
BF16 = mybir.dt.bfloat16
F16 = mybir.dt.float16
ALU = mybir.AluOpType
ACT = mybir.ActivationFunctionType
AX = mybir.AxisListType
ds = bass.ds

P = 128
B, T, D = 4, 1024, 256
H, HD = 16, 16
NL = 2
NTOK = B * T
NT = NTOK // P
BLK = 512
NBLK = NTOK // BLK
TPB = BLK // P
KD = D // P
EPS = 1e-5
NEG = -(2.0 ** 100)

NE, NSH, TOPK, HID = 32, 2, 6, 176
NCH = 11
NG = NE * HID // (NCH * P)
NCS = 3
CHUNKS = NG * NCH + NCS
HIDS = CHUNKS * P
GROUPS = [NCH] * NG + [NCS]

HG = 4
NU = B * H // HG
NQB = T // P
SROWS = 68
MROWS = 66

NPHASE = 7
ENGINES = 5


def max_jobs():
    jobs = []
    for i in range(NQB):
        first = 0
        if i >= 4:
            jobs += [(i, 0, BLK, [h]) for h in range(HG)]
            first = BLK
        w = (i + 1) * P - first
        per = min(HG, BLK // w)
        jobs += [(i, first, w, list(range(h, min(h + per, HG)))) for h in range(0, HG, per)]
    return jobs


def slot_age(c, chunks, ring):
    if c >= ring:
        return ring
    return c + chunks - max(k for k in range(chunks) if k % ring == c % ring)


def raw_count(L, g, c):
    if isinstance(g, int):
        return 32 * (L * 9 + 9)
    if c < 3:
        return 32 * (L * 9 + g * 2 + 1)
    if c >= 8:
        return 32 * (L * 9 + g * 2 + 2)
    return 32 * (L * 4 + g + 1)


def stack_count(L, turn, r):
    return (L * (6, 5, 5)[r] + turn + 1) * 112


def exp_slots():
    return [(qt, kb, BLK if kb < 4 * qt else BLK - (kb - 4 * qt) * P)
            for qt in range(T // BLK) for kb in range(4 * qt + 4)]


MAX_JOBS = max_jobs()
SLOTS = exp_slots()
NJ, NS = len(MAX_JOBS), len(SLOTS)
LATE_JOBS = 4
STEP_LINKS = 5
CHAIN = 133
PRODUCTS = ((0, 0), (0, 1), (1, 0))
Q_SCALE = HD ** -0.5


def build(nc, a, out):
    qks = nc.dram_tensor("qks_scratch", (2, 2, NU, 64, T), F32, kind="Internal").ap()
    vds = nc.dram_tensor("v_scratch", (NU, P, NQB, HG * 32), F32, kind="Internal").ap()

    rows_scratch = nc.dram_tensor("rows_scratch", (NL, 2, SROWS - 48, T), F32, kind="Internal").ap()

    ctx = ExitStack()
    with ctx:
        def sb(name, shape, dt):
            return ctx.enter_context(nc.sbuf_tensor(name, shape, dt))

        def sem(name):
            return ctx.enter_context(nc.semaphore(name))

        split = sb("split", [P, 30720], F32R)
        xT = split[:, 0:16384].rearrange("p (k s t) -> p k s t", k=KD, s=2)
        wreg = split[:, 16384:27648]
        hsp = split[:, 27648:30720].rearrange("p (r s t) -> p r s t", r=3, s=2)
        stack = split[:, 0:24576].rearrange("p (r o h t) -> p r o h t", r=3, o=2, h=HG)
        stack32 = stack.bitcast(F32)
        vreg = split[:, 24576:27648].bitcast(F32).rearrange("p (r t h c) -> p r t h c", r=3, t=NQB, h=HG)
        wqkv = wreg[:, 0:3072].rearrange("p (m k s n) -> p m k s n", m=3, k=KD, s=2)
        qkst = wreg[:, 3072:11264].rearrange("p (r m s f t) -> p r m s f t", r=2, m=2, s=2, f=2)
        w1s = wreg.rearrange("p (c j) -> p c j", j=1024)[:, :, 0:512].rearrange(
            "p c (k s n) -> p c k s n", k=KD, s=2)
        w2s = wreg.rearrange("p (c j) -> p c j", j=1024)[:, :, 512:1024].rearrange(
            "p c (s n) -> p c s n", s=2)

        x = sb("x", [P, NT * D], F32)
        work = sb("work", [P, 12288], F32)
        attn = work[:, 0:8192].rearrange("p (u t c) -> p u t c", u=NU, t=NQB)
        pexp = work[:, 8192:12288].rearrange("p (r h t) -> p r h t", r=4, h=2)
        xn = work[:, 8192:10240].rearrange("p (r t d) -> p r t d", r=2, t=TPB)
        fqk = work[:, 0:2048].rearrange("p (r f t) -> p r f t", r=2, f=2)
        vst = work[:, 2048:6144].rearrange("p (r t h c) -> p r t h c", r=2, t=TPB, h=H)
        vf = work[:, 6144:8192].rearrange("p (r f t) -> p r f t", r=2, f=2)
        mask32 = work[:, 0:2 * P].rearrange("p (m k) -> p m k", m=2)
        wraw = work[:, 10240:11776].rearrange("p (m k n) -> p m k n", m=3, k=KD)
        mtok = work[:, 8192:10240].rearrange("p (r t d) -> p r t d", r=2, t=TPB)
        mT = work[:, 10240:12288].rearrange("p (r k t) -> p r k t", r=2, k=KD)
        gT = work[:, 0:2048].bitcast(BF16)
        sel = work[:, 2048:2048 + HIDS // 2].bitcast(F16)
        hbuf = work[:, 5120:6656].rearrange("p (r t) -> p r t", r=3)
        ysb = work[:, 6656:7680].rearrange("p (f t) -> p f t", f=KD)
        raw = work[:, 7680:11776].rearrange("p (r n) -> p r n", r=8)
        b2s = work[:, 11776:12160].bitcast(BF16).rearrange("p (s d) -> p s d", s=3)
        lgt = work[:, 5120:6208].rearrange("p (t e) -> p t e", e=NE + 2)
        prb = work[:, 6208:7296].rearrange("p (t e) -> p t e", e=NE + 2)
        rep = work[:, 7296:8384].rearrange("p (t e) -> p t e", e=NE + 2)
        gst = work[:, 8384:10432].bitcast(BF16).rearrange("p (t c) -> p t c", c=P)
        lgT = work[:, 10432:11456].rearrange("p (r t) -> p r t", r=2)
        top = work[:, 11456:11712].rearrange("p (t e) -> p t e", e=8)
        b2f = work[:, 5120:5888].rearrange("p (s d) -> p s d", s=3)

        osb = sb("osb", [P, BLK], F32)
        wo = osb
        stat = work[:, 11776:11968].rearrange("p (t s) -> p t s", s=6)
        sv = work[:, 11968:12288].rearrange("p (s t) -> p s t", s=10)
        small = sb("small", [P, 600], F32)
        mpart = small[:, 0:64].rearrange("p (s c) -> p s c", s=2)
        mneg = small[:, 64:96]
        mtr = small[:, 96:128]
        mhl = sb("mhl", [P, 3, 2, 32], F32R)
        rden = small[:, 192:208]
        bqkv = small[:, 208:214]
        bq4 = small[:, 214:216]
        b1 = small[:, 216:216 + CHUNKS]
        rb = small[:, 264:265]
        bo = small[:, 272:528]
        mx8 = small[:, 528:560]
        sm8 = small[:, 560:592]
        ident = sb("ident", [P, P], F32)
        identb = sb("identb", [P, P], BF16)
        maskq = sb("maskq", [P, P], BF16)
        maskk = sb("maskk", [P, P], BF16)

        ps = ctx.enter_context(nc.psum_tensor("ps", [P, 8, BLK], F32))

        s_const, s_x, s_phase = sem("const_loaded"), sem("x_loaded"), sem("phase_done")
        s_apart = sem("wait_carrier")
        s_chain = sem("dve_chain")
        s_var, s_sd = sem("var_ready"), sem("sd_ready")
        s_xn, s_tp, s_xh, s_xl = sem("xn_ready"), sem("xT_psum_ready"), sem("xT_hi_done"), sem("xT_lo_done")
        s_wload, s_wsplit = sem("qkv_weights_loaded"), sem("qkv_weights_split")
        s_pj, s_pf = sem("proj_ready"), sem("proj_evacuated")
        s_ph, s_pl, s_pd = sem("qk_hi_done"), sem("qk_lo_done"), [sem(f"qk_stored{r}") for r in range(2)]
        s_vt, s_vs, s_vd = sem("v_transposed"), sem("v_staged"), [sem(f"v_stored{r}") for r in range(2)]
        s_rows = sem("constant_rows_loaded")
        s_stk = [sem(f"stack_loaded{r}") for r in range(3)]
        s_st, s_pe, s_pv = sem("scoresT_ready"), sem("exp_done"), sem("values_done")
        s_mj, s_mr = sem("scores_ready"), sem("max_done")
        s_mt, s_mrow = sem("neg_max_split"), sem("neg_max_rows_loaded")
        s_ov, s_ot, s_on = sem("out_evacuated"), sem("out_transposed"), sem("out_normalised")
        s_bo, s_bod = sem("merge_bias_loaded"), sem("merge_bias_added")
        s_mc, s_mtp, s_mev, s_mo, s_ma = (sem("merge_tokens_copied"), sem("merge_transposed"),
                                          sem("merge_evacuated"), sem("merge_product"), sem("merge_added"))
        s_rld, s_rsp = sem("router_loaded"), sem("router_split")
        s_lg, s_lge, s_lgt, s_lgd = (sem("logitsT_ready"), sem("logitsT_evacuated"),
                                     sem("logits_transposed"), sem("logits_stored"))
        s_le, s_ee, s_gs, s_gt, s_gd = (sem("logits_shifted"), sem("logits_exp"), sem("gates_split"),
                                        sem("gates_transposed"), sem("gatesT_stored"))
        s_raw = [sem(f"expert_raw_loaded{r}") for r in range(8)]
        s_wh, s_wl = sem("expert_hi_done"), sem("expert_lo_done")
        s_m2 = sem("chunk_summed")
        s_g, s_h, s_r, s_hg, s_hi, s_lo = (sem("gate_rows_ready"), sem("hidden_ready"), sem("relu_done"),
                                           sem("gated_done"), sem("hidden_hi_done"), sem("hidden_lo_done"))
        s_ye, s_yt, s_ya = sem("out_copied"), sem("outT_ready"), sem("out_added")
        s_out = sem("result_stored")
        block = ctx.enter_context(nc.Block())

        def apart(e):
            e.sem_inc(s_apart, 1)

        def phase_end(e, L, n):
            apart(e)
            e.drain().then_inc(s_phase, 1)
            e.wait_ge(s_phase, (L * NPHASE + n + 1) * ENGINES)
            apart(e)

        @block.sync
        def _(sp):
            sp.dma_start(ident[:, :], a["ident"]).then_inc(s_const, 16)
            sp.dma_start(mask32, a["masks"].rearrange("m p k -> p m k")).then_inc(s_const, 16)
            sp.dma_start(rows_scratch, a["rows"]).then_inc(s_const, 16)
            xv = x[:, :].rearrange("p (t d) -> p t d", d=D)
            xin = a["x"].rearrange("b (t p) d -> p (b t) d", p=P)
            for q in range(4):
                sp.dma_start(xv[:, 8 * q:8 * q + 8, :], xin[:, 8 * q:8 * q + 8, :]).then_inc(s_x, 16)

            with sp.Fori(0, NL) as L:
                for m in range(3):
                    sp.dma_start(wraw[:, m], a["wqkv"][L, m].rearrange("(k p) n -> p k n", p=P)).then_inc(s_wload, 16)
                sp.dma_start(bqkv, a["bqkv"][L]).then_inc(s_wload, 16)
                sp.dma_start(bo, a["bo"][ds(L, 1)].partition_broadcast(P).rearrange("p o d -> p (o d)")).then_inc(s_bo, 16)
                phase_end(sp, L, 0)
                with sp.Fori(0, B) as b:
                    for r in range(2):
                        n = L * NBLK + b * 2 + r
                        sp.wait_ge(s_pl, n * 4 + 4 + 4)
                        apart(sp)
                        for m in range(2):
                            for s in range(2):
                                sp.dma_start(
                                    qks[m, s, ds(b * HG, HG), :, r * BLK:(r + 1) * BLK]
                                    .rearrange("(f e) w t -> (e w) f t", f=2),
                                    qkst[:, r, m, s].bitcast(F32)).then_inc(s_pd[r], 16)
                        sp.wait_ge(s_vs, n + 1 + 1)
                        for u in range(HG):
                            sp.dma_start(
                                vds[b * HG + u, :, r * TPB:(r + 1) * TPB, :],
                                vst[:, r, :, HG * u:HG * u + HG, :].rearrange("p t h c -> p t (h c)")
                            ).then_inc(s_vd[r], 16)
                for r in range(2):
                    sp.wait_ge(s_pd[r], (L * B + B) * 64 + 64)
                    sp.wait_ge(s_vd[r], (L * B + B) * 64 + 64)
                phase_end(sp, L, 1)

                sp.wait_ge(s_const, 48)
                for r in range(3):
                    for o in range(2):
                        for h in range(HG):
                            sp.dma_start(stack32[48:SROWS, r, o, h, :], rows_scratch[L, o]).then_inc(s_rows, 16)
                sp.wait_ge(s_rows, (L + 1) * 16 * 24)

                def load_unit(u, r, again=True):
                    if again:
                        sp.wait_ge(s_pv, (L * NU + u - 2) * NS + 2)
                    for o in range(2):
                        for g, s in enumerate(((0, 0, 1), (0, 1, 0))[o]):
                            sp.dma_start(stack32[16 * g:16 * g + 16, r, o],
                                         qks[o, s, u].rearrange("(h w) t -> w h t", h=HG)).then_inc(s_stk[r], 16)
                    sp.dma_start(vreg[:, r], vds[u].rearrange("p t (h c) -> p t h c", h=HG)).then_inc(s_stk[r], 16)

                def load_neg_max(u, r):
                    sp.wait_ge(s_mt, L * NU + u + 1)
                    for s in range(2):
                        for q in range(4):
                            row = stack32[66 + s:67 + s, r, 0].rearrange("p h t -> p (h t)")
                            row = row.rearrange("p (c q w) -> p q c w", q=4, w=32)[:, q]
                            sp.dma_start(row, mhl[32 * q:32 * q + 32, r, s, :].bitcast(F32)).then_inc(s_mrow, 16)

                for u in range(3):
                    load_unit(u, u, again=False)
                load_neg_max(0, 0)
                with sp.Fori(0, 4) as i:
                    for r in range(3):
                        load_neg_max(i * 3 + r + 1, (r + 1) % 3)
                        load_unit(i * 3 + r + 3, r)
                load_neg_max(13, 1)
                load_unit(15, 0)
                load_neg_max(14, 2)
                load_neg_max(15, 0)
                phase_end(sp, L, 2)
                sp.dma_start(wo[:, :].rearrange("p (k n) -> p k n", k=KD),
                             a["wo"][L].rearrange("(k p) n -> p k n", p=P)).then_inc(s_bo, 16)
                phase_end(sp, L, 3)

                sp.dma_start(raw[:, 0, 0:256].rearrange("p (k n) -> p k n", k=KD),
                             a["rw"].rearrange("(k p) n -> p k n", p=P)).then_inc(s_rld, 16)
                sp.dma_start(rb, a["rb"]).then_inc(s_rld, 16)
                sp.dma_start(b1, a["b1"]).then_inc(s_rld, 16)
                sp.dma_start(sel, a["sel"]).then_inc(s_rld, 16)
                phase_end(sp, L, 4)
                sp.wait_ge(s_gs, (L + 1) * 1)
                for s in range(3):
                    sp.dma_start(b2f[32 * s:32 * s + 32, 0, :], a["b2"][0:NE]).then_inc(s_rld, 16)
                sp.dma_start(b2f[96:128, 0, :], a["b2"][NE:NE + 32]).then_inc(s_rld, 16)
                phase_end(sp, L, 5)

                def load_chunk(col, c, n):
                    r = c % 8
                    sp.wait_ge(s_wl, n)
                    sp.dma_start(raw[:, r, 0:256].rearrange("p (k n) -> p k n", k=KD),
                                 a["w1"][:, ds(col, P)].rearrange("(k p) n -> p k n", p=P)).then_inc(s_raw[r], 16)
                    sp.dma_start(raw[:, r, 256:512], a["w2"][ds(col, P), :]).then_inc(s_raw[r], 16)

                with sp.Fori(0, NG) as g:
                    for c in range(NCH):
                        n = L * CHUNKS + g * NCH + c
                        n = n - 8 if c >= 8 else (n + 8 - NCH if c + 8 < NCH else n - NCH)
                        load_chunk((g * NCH + c) * P, c, n + 1 + 11)
                for c in range(NCS):
                    load_chunk((NG * NCH + c) * P, c, L * CHUNKS + NG * NCH + c + 8 - NCH + 1 + 11)
                phase_end(sp, L, 6)

            xo = out.rearrange("b (t p) d -> p (b t) d", p=P)
            for q in range(4):
                sp.dma_start(xo[:, 8 * q:8 * q + 8, :], xv[:, 8 * q:8 * q + 8, :]).then_inc(s_out, 16)
            sp.wait_ge(s_out, 64)

        @block.vector
        def _(dve):
            v = nc.vector
            dve.sem_inc(s_xl, 2)
            dve.sem_inc(s_vs, 1)
            dve.sem_inc(s_mr, 2)
            dve.sem_inc(s_on, 1)
            dve.sem_inc(s_ma, 2)
            dve.sem_inc(s_lgd, 2)
            dve.sem_inc(s_gd, 2)
            dve.sem_inc(s_hg, 2)
            dve.sem_inc(s_ya, 1)
            chain = [0]
            turns = [0]

            def link(ins):
                chain[0] += 1
                ins.then_inc(s_chain, 1)

            dve.wait_ge(s_const, 48)
            v.tensor_copy(identb[:, :], ident[:, :])
            v.tensor_copy(maskq[:, :], mask32[:, 0, :])
            v.tensor_copy(maskk[:, :], mask32[:, 1, :])
            dve.wait_ge(s_x, 64)

            with dve.Fori(0, NL) as L:
                chain[0] = 0

                def linked():
                    dve.wait_ge(s_chain, L * CHAIN + turns[0] + chain[0])

                def norm(k):
                    with dve.Fori(0, NT // 4) as t:
                        for j in range(4):
                            last = v.bn_stats(stat[:, ds(t * 4 + j, 1), :].rearrange("p t s -> p (t s)"),
                                              x[:, ds((t * 4 + j) * D, D)])
                        last.then_inc(s_chain, 1)
                    chain[0] += NT // 4
                    linked()
                    me, ve, mo, vo = (stat[:, :, s] for s in (1, 2, 4, 5))
                    v.tensor_tensor(sv[:, 0], me, mo, ALU.subtract)
                    v.tensor_tensor(sv[:, 1], me, mo, ALU.add)
                    link(v.tensor_tensor(sv[:, 2], ve, vo, ALU.add))
                    linked()
                    v.tensor_tensor(sv[:, 3], sv[:, 0], sv[:, 0], ALU.mult)
                    link(v.tensor_scalar(sv[:, 4], sv[:, 2], 1.0 / D, EPS, ALU.mult, ALU.add))
                    linked()
                    v.scalar_tensor_tensor(sv[:, 5], sv[:, 3], 0.25, sv[:, 4], ALU.mult, ALU.add).then_inc(s_var, 1)
                    dve.wait_ge(s_sd, k + 1)
                    link(v.reciprocal(sv[:, 7], sv[:, 6]))
                    linked()
                    link(v.tensor_tensor(sv[:, 7], sv[:, 5], sv[:, 7], ALU.mult))
                    linked()
                    link(v.tensor_tensor(sv[:, 7], sv[:, 6], sv[:, 7], ALU.add))
                    linked()
                    link(v.reciprocal(sv[:, 7], sv[:, 7]))
                    linked()
                    link(v.tensor_scalar(sv[:, 8], sv[:, 7], 2.0, None, ALU.mult))
                    linked()
                    link(v.scalar_tensor_tensor(sv[:, 9], sv[:, 1], -0.5, sv[:, 8], ALU.mult, ALU.mult))
                    linked()
                    apart(dve)
                    with dve.Fori(0, NBLK // 2) as i:
                        for r in range(2):
                            n = k * NBLK + i * 2 + r
                            dve.wait_ge(s_tp, n + 1)
                            for j in range(TPB):
                                t = (i * 2 + r) * TPB + j
                                last = v.tensor_scalar(xn[:, r, j, :], x[:, ds(t * D, D)], sv[:, 8, ds(t, 1)],
                                                       sv[:, 9, ds(t, 1)], ALU.mult, ALU.add)
                            last.then_inc(s_xn, 1)
                        for r in range(2):
                            n = k * NBLK + i * 2 + r
                            dve.wait_ge(s_xh, n + 1)
                            col = ds((i * 2 + r) * BLK, BLK)
                            v.tensor_tensor(xT[:, :, 1, col], ps[:, 2 * r:2 * r + 2, :],
                                            xT[:, :, 0, col].bitcast(F32), ALU.subtract).then_inc(s_xl, 1)

                norm(L * 2)
                phase_end(dve, L, 0)

                dve.wait_ge(s_wload, (L + 1) * 64)
                v.tensor_scalar(bq4, bqkv[:, 0:2], HD ** -0.5, None, ALU.mult)
                link(v.tensor_copy(wqkv[:, :, :, 0, :], wraw))
                linked()
                v.tensor_tensor(wqkv[:, :, :, 1, :], wraw, wqkv[:, :, :, 0, :].bitcast(F32),
                                ALU.subtract).then_inc(s_wsplit, 1)
                v.memset(vst[:, :, :, :, HD:32], 1.0)
                with dve.Fori(0, B) as b:
                    for r in range(2):
                        n = L * NBLK + b * 2 + r
                        dve.wait_ge(s_pd[r], (L * B + b) * 64 + 64)
                        for m in range(2):
                            for f in range(2):
                                dve.wait_ge(s_pf, n * 6 + m * 2 + f + 1 + 3)
                                v.tensor_copy(qkst[:, r, m, 0, f], fqk[:, m, f]).then_inc(s_ph, 1)
                        dve.wait_ge(s_vd[r], (L * B + b) * 64 + 64)
                        dve.wait_ge(s_vt, n + 1 + 2)
                        for f in range(2):
                            last = v.tensor_copy(vst[:, r, :, 8 * f:8 * f + 8, 0:HD],
                                                 ps[:, 6 + f, :].rearrange("p (t h c) -> p t h c", t=TPB, h=8))
                        last.then_inc(s_vs, 1)
                phase_end(dve, L, 1)

                def max_job(n, j):
                    i, first, w, heads = MAX_JOBS[j]
                    dve.wait_ge(s_mj, n * NJ + j + 1)
                    cols = mpart[:, 0 if first or i < 4 else 1, :].rearrange("p (h q) -> p h q", h=HG)
                    v.tensor_reduce(cols[:, heads[0]:heads[0] + len(heads), i],
                                    ps[:, 4 + j % 2, 0:w * len(heads)].rearrange("p (h k) -> p h k", k=w),
                                    AX.X, ALU.max, negate=True).then_inc(s_mr, 1)

                def split_max(u, r, n):
                    late = mpart[:, :, :].rearrange("p s (h q) -> p s h q", h=HG)
                    neg = mneg.rearrange("p (h q) -> p h q", h=HG)
                    dve.wait_ge(s_mr, n * NJ + NJ + 2)
                    v.tensor_copy(neg[:, :, 0:4], late[:, 0, :, 0:4])
                    link(v.tensor_tensor(neg[:, :, 4:8], late[:, 0, :, 4:8], late[:, 1, :, 4:8], ALU.min))
                    linked()
                    link(v.transpose(mtr, mneg))
                    linked()
                    link(v.tensor_copy(mhl[:, r, 0, :], mtr))
                    linked()
                    v.tensor_tensor(mhl[:, r, 1, :], mtr, mhl[:, r, 0, :].bitcast(F32),
                                    ALU.subtract).then_inc(s_mt, 1)

                def normalise(u, qt):
                    dve.wait_ge(s_ot, (L * NU + u) * 2 + qt + 1 + 1)
                    o = ps[:, 7, :].rearrange("p (q h c) -> p q h c", q=4, h=HG)
                    rd = rden.rearrange("p (q h) -> p q h", q=4)
                    link(v.reciprocal(rd, o[:, :, :, HD]))
                    linked()
                    v.tensor_tensor(
                        attn[:, ds(u, 1), 4 * qt:4 * qt + 4, :].rearrange("p u t (h c) -> p (u t h) c", h=HG),
                        o[:, :, :, 0:HD].rearrange("p q h c -> p (q h) c"),
                        rden.unsqueeze(2).broadcast_to([P, 16, HD]), ALU.mult).then_inc(s_on, 1)

                def step(u, r, first=False, ahead=True):
                    if ahead:
                        for j in range(NJ):
                            if j == NJ * 8 // NS:
                                normalise(u, 0)
                            max_job(L * NU + u + 1, j)
                        split_max(u + 1, (r + 1) % 3, L * NU + u + 1)
                    else:
                        normalise(u, 0)
                    normalise(u, 1)

                for j in range(NJ):
                    max_job(L * NU, j)
                split_max(0, 0, L * NU)
                with dve.Fori(0, 5) as i:
                    before = chain[0]
                    turns[0] = i * (3 * STEP_LINKS)
                    for r in range(3):
                        step(i * 3 + r, r)
                    turns[0] = 0
                    assert chain[0] == before + 3 * STEP_LINKS
                chain[0] += 4 * 3 * STEP_LINKS
                step(15, 0, ahead=False)
                phase_end(dve, L, 2)

                with dve.Fori(0, NBLK // 2) as i:
                    for r in range(2):
                        n = L * NBLK + i * 2 + r
                        dve.wait_ge(s_mtp, n + 1)
                        for g in range(HG):
                            last = v.tensor_copy(mtok[:, r, :, 64 * g:64 * g + 64],
                                                 attn[:, ds((i * HG) + g, 1), TPB * r:TPB * r + TPB, :]
                                                 .rearrange("p u t c -> p (u t) c"))
                        last.then_inc(s_mc, 1)
                    for r in range(2):
                        n = L * NBLK + i * 2 + r
                        dve.wait_ge(s_mo, n + 1 + 2)
                        if r == 0:
                            dve.wait_ge(s_bod, (L + 1) * NT)
                        xb = x[:, ds((i * 2 + r) * TPB * D, TPB * D)]
                        v.tensor_tensor(xb, ps[:, 4 + 2 * r:6 + 2 * r, :].rearrange("p f t -> p (f t)"), xb,
                                        ALU.add).then_inc(s_ma, 1)
                phase_end(dve, L, 3)
                norm(L * 2 + 1)
                dve.wait_ge(s_rld, L * 128 + 64)
                link(v.tensor_copy(hsp[:, 0, 0, 0:256], raw[:, 0, 0:256]))
                linked()
                v.tensor_tensor(hsp[:, 0, 1, 0:256], raw[:, 0, 0:256], hsp[:, 0, 0, 0:256].bitcast(F32), ALU.subtract)
                phase_end(dve, L, 4)

                with dve.Fori(0, NBLK // 2) as i:
                    for r in range(2):
                        n = L * NBLK + i * 2 + r
                        dve.wait_ge(s_lgt, n + 1 + 2)
                        v.tensor_copy(lgt[:, ds((i * 2 + r) * TPB, TPB), 0:NE],
                                      ps[:, 2 + r, 0:TPB * NE].rearrange("p (t e) -> p t e", e=NE)).then_inc(s_lgd, 1)
                dve.wait_ge(s_lgd, (L + 1) * NBLK + 2)
                link(v.tensor_reduce(mx8, lgt[:, :, 0:NE], AX.X, ALU.max))
                linked()
                v.tensor_tensor(lgt[:, :, 0:NE], lgt[:, :, 0:NE], mx8.unsqueeze(2).broadcast_to([P, NT, NE]),
                                ALU.subtract).then_inc(s_le, 1)
                dve.wait_ge(s_ee, L + 1)
                v.memset(prb[:, :, NE:NE + 2], -1.0)
                link(v.tensor_reduce(sm8, rep[:, :, 0:NE], AX.X, ALU.add))
                linked()
                link(v.reciprocal(sm8, sm8))
                linked()
                link(v.tensor_tensor(prb[:, :, 0:NE], rep[:, :, 0:NE], sm8.unsqueeze(2).broadcast_to([P, NT, NE]),
                                     ALU.mult))
                linked()
                apart(dve)
                for t in range(NT):
                    last = v.max(top[:, t, :], prb[:, t, :])
                link(last)
                linked()
                link(v.memset(top[:, :, TOPK:8], -1.0))
                linked()
                apart(dve)
                for t in range(NT):
                    last = v.match_replace(rep[:, t, :], top[:, t, :], prb[:, t, :], 0.0)
                link(last)
                linked()
                g = lgt[:, :, 0:NE]
                link(v.tensor_tensor(g, prb[:, :, 0:NE], rep[:, :, 0:NE], ALU.subtract))
                linked()
                link(v.tensor_reduce(sm8, g, AX.X, ALU.add))
                linked()
                link(v.reciprocal(sm8, sm8))
                linked()
                link(v.tensor_tensor(g, g, sm8.unsqueeze(2).broadcast_to([P, NT, NE]), ALU.mult))
                linked()
                v.memset(gst[:, :, 3 * NE:P], 0.0)
                link(v.tensor_copy(gst[:, :, 0:NE], g))
                linked()
                v.memset(gst[:, :, 3 * NE:3 * NE + NSH], 1.0 / NSH)
                link(v.tensor_tensor(g, g, gst[:, :, 0:NE], ALU.subtract))
                linked()
                link(v.tensor_copy(gst[:, :, NE:2 * NE], g))
                linked()
                link(v.tensor_tensor(g, g, gst[:, :, NE:2 * NE], ALU.subtract))
                linked()
                v.tensor_copy(gst[:, :, 2 * NE:3 * NE], g).then_inc(s_gs, 1)
                for n in range(NBLK):
                    dve.wait_ge(s_gt, L * NBLK + n + 1)
                    v.tensor_copy(gT[:, n * BLK:(n + 1) * BLK],
                                  ps[:, n % 2, 0:BLK // 2].bitcast(BF16)).then_inc(s_gd, 1)
                dve.wait_ge(s_rld, L * 128 + 128)
                link(v.tensor_copy(b2s[:, 0, :], b2f[:, 0, :]))
                linked()
                link(v.tensor_tensor(b2f[:, 1, :], b2f[:, 0, :], b2s[:, 0, :], ALU.subtract))
                linked()
                link(v.tensor_copy(b2s[:, 1, :], b2f[:, 1, :]))
                linked()
                link(v.tensor_tensor(b2f[:, 2, :], b2f[:, 1, :], b2s[:, 1, :], ALU.subtract))
                linked()
                v.tensor_copy(b2s[:, 2, :], b2f[:, 2, :])
                phase_end(dve, L, 5)

                def gate_mul(n, c):
                    dve.wait_ge(s_r, n + c + 1 + 3)
                    dve.wait_ge(s_g, n + c + 1)
                    v.tensor_tensor(hbuf[:, c % 3, :], ps[:, 3 + c % 2, :], hbuf[:, c % 3, :],
                                    ALU.mult).then_inc(s_hg, 1)

                def hidden_hi(n, c, chunks):
                    dve.wait_ge(s_hg, n + c + 1 + 2)
                    dve.wait_ge(s_m2, n + c + 4 - slot_age(c, chunks, 3))
                    v.tensor_copy(hsp[:, c % 3, 0, :], hbuf[:, c % 3, :]).then_inc(s_hi, 1)

                def out_add(yn, blk, f):
                    dve.wait_ge(s_yt, yn * 2 + f + 1 + 1)
                    xb = x[:, ds(blk * TPB * D + f * 512, 512)]
                    v.tensor_tensor(xb, ps[:, 7, :], xb, ALU.add).then_inc(s_ya, 1)

                def group(g, chunks, first_n, first_y, first_w):
                    def blk_body(blk, lagged, split_w):
                        n = first_n + blk * chunks
                        for c in range(chunks):
                            if split_w:
                                dve.wait_ge(s_raw[c % 8], first_w(c))
                                v.tensor_copy(w1s[:, c, :, 0, :],
                                              raw[:, c % 8, 0:256].rearrange("p (k n) -> p k n", k=KD))
                                v.tensor_copy(w2s[:, c, 0, :], raw[:, c % 8, 256:512]).then_inc(s_wh, 1)
                            gate_mul(n, c)
                            hidden_hi(n, c, chunks)
                            if lagged and c == 2:
                                out_add(first_y + blk - 1, blk - 1, 0)
                            if lagged and c == min(chunks - 1, 4):
                                out_add(first_y + blk - 1, blk - 1, 1)
                    blk_body(0, False, True)
                    with dve.Fori(1, NBLK) as blk:
                        blk_body(blk, True, False)
                    out_add(first_y + NBLK - 1, NBLK - 1, 0)
                    out_add(first_y + NBLK - 1, NBLK - 1, 1)

                with dve.Fori(0, NG) as g:
                    group(g, NCH, L * CHUNKS * NBLK + g * NCH * NBLK, L * (NG + 1) * NBLK + g * NBLK,
                          lambda c: raw_count(L, g, c))
                group(NG, NCS, L * CHUNKS * NBLK + NG * NCH * NBLK, L * (NG + 1) * NBLK + NG * NBLK,
                      lambda c: raw_count(L, NG, c))
                phase_end(dve, L, 6)
            assert chain[0] == CHAIN, chain[0]

        @block.scalar
        def _(act):
            c = nc.scalar
            act.sem_inc(s_pf, 3)
            act.sem_inc(s_pe, 2)
            act.sem_inc(s_ov, 1)
            act.sem_inc(s_mev, 2)
            act.sem_inc(s_lge, 2)
            act.sem_inc(s_r, 3)
            act.sem_inc(s_ye, 1)
            with act.Fori(0, NL) as L:
                def norm(k):
                    act.wait_ge(s_var, k + 1)
                    c.activation(sv[:, 6], sv[:, 5], ACT.Sqrt).then_inc(s_sd, 1)
                    with act.Fori(0, NBLK // 2) as i:
                        for r in range(2):
                            act.wait_ge(s_tp, k * NBLK + i * 2 + r + 1 + 2)
                            c.activation(xT[:, :, 0, ds((i * 2 + r) * BLK, BLK)], ps[:, 2 * r:2 * r + 2, :],
                                         ACT.Copy).then_inc(s_xh, 1)

                norm(L * 2)
                phase_end(act, L, 0)

                act.wait_ge(s_wsplit, L + 1)
                with act.Fori(0, B) as b:
                    for r in range(2):
                        n = L * NBLK + b * 2 + r
                        for m in range(3):
                            for f in range(2):
                                j = m * 2 + f
                                act.wait_ge(s_pj, n * 6 + j + 1)
                                if m < 2:
                                    act.wait_ge(s_pl, n * 4 + j + 1)
                                elif f == 0:
                                    act.wait_ge(s_vt, n + 1)
                                c.activation(fqk[:, m, f] if m < 2 else vf[:, r, f], ps[:, j % 3, :], ACT.Identity,
                                             bias=bq4[:, f:f + 1] if m == 0 else bqkv[:, j:j + 1],
                                             scale=Q_SCALE if m == 0 else 1.0).then_inc(s_pf, 1)
                phase_end(act, L, 1)

                def evacuate(U, qt):
                    act.wait_ge(s_pv, U * NS + (4, NS)[qt] + 2)
                    act.wait_ge(s_ot, U * 2 + qt + 1)
                    c.activation(osb[:, :], ps[:, 6, :], ACT.Copy).then_inc(s_ov, 1)

                def step(u):
                    U = L * NU + u
                    for s, (qt, kb, w) in enumerate(SLOTS):
                        act.wait_ge(s_pv, U * NS + s + 1)
                        for h in range(2):
                            act.wait_ge(s_st, (U * NS + s) * 2 + h + 1)
                            c.activation(pexp[:, (s % 2) * 2 + h, :, BLK - w:], ps[:, 2 * h:2 * h + 2, BLK - w:],
                                         ACT.Exp).then_inc(s_pe, 1)
                        if s == 4:
                            evacuate(U, 0)
                    evacuate(U, 1)

                with act.Fori(0, 8) as i:
                    for r in range(2):
                        step(i * 2 + r)
                phase_end(act, L, 2)

                with act.Fori(0, NBLK // 2) as i:
                    for r in range(2):
                        n = L * NBLK + i * 2 + r
                        act.wait_ge(s_mtp, n + 1 + 2)
                        act.wait_ge(s_mo, n + 1)
                        c.activation(mT[:, r], ps[:, 2 * r:2 * r + 2, :], ACT.Copy).then_inc(s_mev, 1)
                phase_end(act, L, 3)
                norm(L * 2 + 1)
                phase_end(act, L, 4)

                act.wait_ge(s_rld, L * 128 + 64)
                with act.Fori(0, NBLK // 2) as i:
                    for r in range(2):
                        n = L * NBLK + i * 2 + r
                        act.wait_ge(s_lg, n + 1)
                        act.wait_ge(s_lgt, n + 1)
                        c.activation(lgT[0:NE, r, :], ps[0:NE, r, :], ACT.Identity,
                                     bias=rb[0:NE, :]).then_inc(s_lge, 1)
                act.wait_ge(s_le, L + 1)
                c.activation(rep[:, :, 0:NE], lgt[:, :, 0:NE], ACT.Exp).then_inc(s_ee, 1)
                phase_end(act, L, 5)

                def group(g, chunks, first_n, first_y):
                    def copy_out(blk):
                        Y = first_y + blk
                        act.wait_ge(s_m2, first_n + blk * chunks + chunks + 3)
                        act.wait_ge(s_yt, Y * 2 + 1)
                        c.activation(ysb, ps[:, 5:7, :], ACT.Copy).then_inc(s_ye, 1)

                    def blk_body(blk, lagged):
                        for k in range(chunks):
                            Q = first_n + blk * chunks + k
                            act.wait_ge(s_h, Q + 1)
                            act.wait_ge(s_lo, Q + 4 - slot_age(k, chunks, 3))
                            apart(act)
                            c.activation(hbuf[:, k % 3, :], ps[:, k % 3, :], ACT.Relu,
                                         bias=b1[:, ds(g * NCH + k, 1)]).then_inc(s_r, 1)
                            if lagged and k == 1:
                                copy_out(blk - 1)
                    blk_body(0, False)
                    with act.Fori(1, NBLK) as blk:
                        blk_body(blk, True)
                    copy_out(NBLK - 1)

                with act.Fori(0, NG) as g:
                    group(g, NCH, L * CHUNKS * NBLK + g * NCH * NBLK, L * (NG + 1) * NBLK + g * NBLK)
                group(NG, NCS, L * CHUNKS * NBLK + NG * NCH * NBLK, L * (NG + 1) * NBLK + NG * NBLK)
                phase_end(act, L, 6)

        @block.gpsimd
        def _(pool):
            p = nc.gpsimd
            pool.sem_inc(s_pl, 4)
            pool.sem_inc(s_wl, 11)
            pool.sem_inc(s_lo, 3)
            for r in range(2):
                pool.sem_inc(s_pd[r], 64)
                pool.sem_inc(s_vd[r], 64)
            with pool.Fori(0, NL) as L:
                phase_end(pool, L, 0)
                with pool.Fori(0, B) as b:
                    for r in range(2):
                        for m in range(2):
                            for f in range(2):
                                pool.wait_ge(s_ph, (L * NBLK + b * 2 + r) * 4 + m * 2 + f + 1)
                                p.tensor_tensor(qkst[:, r, m, 1, f], fqk[:, m, f], qkst[:, r, m, 0, f].bitcast(F32),
                                                ALU.subtract).then_inc(s_pl, 1)
                phase_end(pool, L, 1)
                pool.wait_ge(s_bo, L * 32 + 16)
                apart(pool)
                with pool.Fori(0, NT) as t:
                    xt = x[:, ds(t * D, D)]
                    p.tensor_tensor(xt, xt, bo, ALU.add).then_inc(s_bod, 1)
                phase_end(pool, L, 2)
                phase_end(pool, L, 3)
                phase_end(pool, L, 4)
                phase_end(pool, L, 5)

                def group(g, chunks, first_n, first_w):
                    def blk_body(blk, split_w):
                        for c in range(chunks):
                            if split_w:
                                pool.wait_ge(s_wh, first_w + c + 1)
                                p.tensor_tensor(w1s[:, c, :, 1, :], raw[:, c % 8, 0:256].rearrange("p (k n) -> p k n", k=KD),
                                                w1s[:, c, :, 0, :].bitcast(F32), ALU.subtract)
                                p.tensor_tensor(w2s[:, c, 1, :], raw[:, c % 8, 256:512], w2s[:, c, 0, :].bitcast(F32),
                                                ALU.subtract).then_inc(s_wl, 1)
                            pool.wait_ge(s_hi, first_n + blk * chunks + c + 1)
                            p.tensor_tensor(hsp[:, c % 3, 1, :], hbuf[:, c % 3, :], hsp[:, c % 3, 0, :].bitcast(F32),
                                            ALU.subtract).then_inc(s_lo, 1)
                    blk_body(0, True)
                    with pool.Fori(1, NBLK) as blk:
                        blk_body(blk, False)

                with pool.Fori(0, NG) as g:
                    group(g, NCH, L * CHUNKS * NBLK + g * NCH * NBLK, L * CHUNKS + g * NCH)
                group(NG, NCS, L * CHUNKS * NBLK + NG * NCH * NBLK, L * CHUNKS + NG * NCH)
                phase_end(pool, L, 6)

        @block.tensor
        def _(pe):
            mm, tr = nc.tensor.matmul, nc.tensor.transpose
            pe.sem_inc(s_tp, 2)
            pe.sem_inc(s_vt, 2)
            pe.sem_inc(s_pv, 2)
            pe.sem_inc(s_ot, 1)
            pe.sem_inc(s_mtp, 2)
            pe.sem_inc(s_mo, 2)
            pe.sem_inc(s_lgt, 2)
            pe.sem_inc(s_m2, 3)
            pe.sem_inc(s_yt, 1)
            pe.wait_ge(s_const, 48)
            with pe.Fori(0, NL) as L:
                def norm(k):
                    with pe.Fori(0, NBLK // 2) as i:
                        for r in range(2):
                            n = k * NBLK + i * 2 + r
                            pe.wait_ge(s_xn, n + 1)
                            pe.wait_ge(s_xl, n + 1)
                            for f in range(KD):
                                for j in range(TPB):
                                    last = tr(ps[:, 2 * r + f, j * P:j * P + P], xn[:, r, j, f * P:f * P + P],
                                              ident[:, :])
                            last.then_inc(s_tp, 1)

                norm(L * 2)
                phase_end(pe, L, 0)

                pe.wait_ge(s_wsplit, L + 1)
                apart(pe)
                with pe.Fori(0, B) as b:
                    for r in range(2):
                        n = L * NBLK + b * 2 + r
                        col = ds((b * 2 + r) * BLK, BLK)
                        for m in range(3):
                            for f in range(2):
                                j = m * 2 + f
                                pe.wait_ge(s_pf, n * 6 + j + 1)
                                for e, (ws, xs) in enumerate(PRODUCTS):
                                    for k in range(KD):
                                        last = mm(ps[:, j % 3, :], wqkv[:, m, k, ws, f * P:f * P + P],
                                                  xT[:, k, xs, col], start=e == 0 and k == 0,
                                                  stop=e == 2 and k == KD - 1)
                                last.then_inc(s_pj, 1)
                        pe.wait_ge(s_pf, n * 6 + 6 + 3)
                        pe.wait_ge(s_vs, n + 1)
                        for f in range(2):
                            for j in range(TPB):
                                last = tr(ps[:, 6 + f, j * P:j * P + P], vf[:, r, f, j * P:j * P + P], ident[:, :])
                        last.then_inc(s_vt, 1)
                phase_end(pe, L, 1)

                def max_job(U, r, j):
                    i, first, w, heads = MAX_JOBS[j]
                    bank = ps[:, 4 + j % 2, 0:w * len(heads)].rearrange("p (h k) -> p h k", k=w)
                    diagonal = first + w == (i + 1) * P
                    pe.wait_ge(s_mr, U * NJ + j + 1)
                    for e, h in enumerate(heads):
                        last = mm(bank[:, e, :], stack[0:MROWS, r, 0, h, i * P:i * P + P],
                                  stack[0:MROWS, r, 1, h, first:first + w], start=e == 0,
                                  stop=not diagonal and e == len(heads) - 1, skip_group_check=True)
                    if diagonal:
                        last = mm(bank[:, :, w - P:w], identb[:, :],
                                  maskq[:, :].unsqueeze(1).broadcast_to([P, len(heads), P]),
                                  start=False, stop=True, skip_group_check=True)
                    last.then_inc(s_mj, 1)

                def scores(U, r, s, half):
                    qt, kb, w = SLOTS[s]
                    pe.wait_ge(s_pe, (U * NS + s) * 2 + half + 1)
                    for e in range(2):
                        h = 2 * half + e
                        last = mm(ps[:, h, BLK - w:], stack[0:SROWS, r, 1, h, kb * P:kb * P + P],
                                  stack[0:SROWS, r, 0, h, (qt + 1) * BLK - w:(qt + 1) * BLK],
                                  start=True, stop=kb < 4 * qt, skip_group_check=True)
                        if kb >= 4 * qt:
                            last = mm(ps[:, h, BLK - w:BLK - w + P], identb[:, :], maskk[:, :], start=False, stop=True,
                                      skip_group_check=True)
                    last.then_inc(s_st, 1)

                def values(U, r, s):
                    qt, kb, w = SLOTS[s]
                    if kb == 0:
                        pe.wait_ge(s_ov, U * 2 + qt + 1)
                    pe.wait_ge(s_pe, (U * NS + s) * 2 + 2 + 2)
                    for h in range(HG):
                        last = mm(ps[32 * h:32 * h + 32, 6, BLK - w:], vreg[:, r, kb, h, :],
                                  pexp[:, (s % 2) * 2 + h // 2, h % 2, BLK - w:], start=kb == 0,
                                  stop=kb == 4 * qt + 3, skip_group_check=True)
                    last.then_inc(s_pv, 1)

                def transpose_out(U, qt):
                    pe.wait_ge(s_ov, U * 2 + qt + 1 + 1)
                    pe.wait_ge(s_on, U * 2 + qt + 1)
                    for j in range(4):
                        last = tr(ps[:, 7, j * P:j * P + P], osb[:, j * P:j * P + P], ident[:, :])
                    last.then_inc(s_ot, 1)

                def step(turn, r, ahead=True):
                    U = L * NU + turn * 3 + r
                    job = 0
                    pe.wait_ge(s_mrow, (U + 1) * 128)
                    if ahead:
                        pe.wait_ge(s_stk[(r + 1) % 3], stack_count(L, turn + (r + 1) // 3, (r + 1) % 3))
                    for s in range(NS):
                        scores(U, r, s, 0)
                        scores(U, r, s, 1)
                        until = (NJ - LATE_JOBS) * (s + 1) // NS if ahead else 0
                        if job < until:
                            max_job(U + 1, (r + 1) % 3, job)
                            job += 1
                        if s:
                            values(U, r, s - 1)
                        while job < until:
                            max_job(U + 1, (r + 1) % 3, job)
                            job += 1
                        if s == 6:
                            transpose_out(U, 0)
                    while ahead and job < NJ - LATE_JOBS // 2:
                        max_job(U + 1, (r + 1) % 3, job)
                        job += 1
                    values(U, r, NS - 1)
                    while ahead and job < NJ:
                        max_job(U + 1, (r + 1) % 3, job)
                        job += 1
                    transpose_out(U, 1)

                pe.wait_ge(s_stk[0], stack_count(L, 0, 0))
                for j in range(NJ):
                    max_job(L * NU, 0, j)
                with pe.Fori(0, 5) as i:
                    for r in range(3):
                        step(i, r)
                step(5, 0, ahead=False)
                phase_end(pe, L, 2)

                pe.wait_ge(s_bo, (L + 1) * 32)
                apart(pe)
                with pe.Fori(0, NBLK // 2) as i:
                    for r in range(2):
                        n = L * NBLK + i * 2 + r
                        pe.wait_ge(s_mc, n + 1)
                        pe.wait_ge(s_mev, n + 1)
                        for f in range(KD):
                            for j in range(TPB):
                                last = tr(ps[:, 2 * r + f, j * P:j * P + P], mtok[:, r, j, f * P:f * P + P],
                                          ident[:, :])
                        last.then_inc(s_mtp, 1)
                    for r in range(2):
                        n = L * NBLK + i * 2 + r
                        pe.wait_ge(s_mev, n + 1 + 2)
                        pe.wait_ge(s_ma, n + 1)
                        for j in range(TPB):
                            for k in range(KD):
                                last = mm(ps[:, 4 + 2 * r + j // 2, (j % 2) * D:(j % 2) * D + D],
                                          mT[:, r, k, j * P:j * P + P], wo[:, k * D:k * D + D],
                                          start=k == 0 and j % 2 == 0, stop=k == KD - 1, skip_group_check=True)
                        last.then_inc(s_mo, 1)
                phase_end(pe, L, 3)
                norm(L * 2 + 1)
                phase_end(pe, L, 4)

                with pe.Fori(0, NBLK // 2) as i:
                    for r in range(2):
                        pe.wait_ge(s_lge, L * NBLK + i * 2 + r + 1)
                        for e, (ws, xs) in enumerate(PRODUCTS):
                            for k in range(KD):
                                last = mm(ps[:, r, :], hsp[:, 0, ws, k * P:k * P + P],
                                          xT[:, k, xs, ds((i * 2 + r) * BLK, BLK)],
                                          start=e == 0 and k == 0, stop=e == 2 and k == KD - 1)
                        last.then_inc(s_lg, 1)
                    for r in range(2):
                        n = L * NBLK + i * 2 + r
                        pe.wait_ge(s_lge, n + 1 + 2)
                        pe.wait_ge(s_lgd, n + 1)
                        apart(pe)
                        for j in range(TPB):
                            last = tr(ps[:, 2 + r, j * NE:j * NE + NE], lgT[0:NE, r, j * P:j * P + P],
                                      ident[0:NE, 0:NE])
                        last.then_inc(s_lgt, 1)
                pe.wait_ge(s_gs, L + 1)
                for n in range(NBLK):
                    pe.wait_ge(s_gd, L * NBLK + n + 1)
                    for j in range(TPB):
                        last = tr(ps[:, n % 2, 64 * j:64 * j + 64].bitcast(BF16), gst[:, n * TPB + j, :], identb[:, :])
                    last.then_inc(s_gt, 1)
                phase_end(pe, L, 5)

                def group(g, chunks, first_n, first_y, first_w):
                    def gate_rows(blk, c):
                        Q = first_n + blk * chunks + c
                        pe.wait_ge(s_hg, Q + 3 - slot_age(c, chunks, 2))
                        mm(ps[:, 3 + c % 2, :], sel[:, ds((g * NCH + c) * P, P)], gT[:, ds(blk * BLK, BLK)],
                           start=True, stop=True).then_inc(s_g, 1)

                    def hidden(blk, c):
                        Q = first_n + blk * chunks + c
                        pe.wait_ge(s_r, Q + 4 - slot_age(c, chunks, 3))
                        for e, (ws, xs) in enumerate(PRODUCTS):
                            for k in range(KD):
                                last = mm(ps[:, c % 3, :], w1s[:, c, k, ws, :], xT[:, k, xs, ds(blk * BLK, BLK)],
                                          start=e == 0 and k == 0, stop=e == 2 and k == KD - 1)
                        last.then_inc(s_h, 1)

                    def summed(blk, c):
                        Q = first_n + blk * chunks + c
                        if c == 0:
                            pe.wait_ge(s_ye, first_y + blk + 1)
                            if chunks == NCS:
                                for f in range(KD):
                                    for s in range(3):
                                        mm(ps[:, 5 + f, :], b2s[:, s, f * P:f * P + P], gT[:, ds(blk * BLK, BLK)],
                                           start=s == 0, stop=False)
                        pe.wait_ge(s_lo, Q + 1 + 3)
                        for f in range(KD):
                            for e, (ws, xs) in enumerate(PRODUCTS):
                                last = mm(ps[:, 5 + f, :], w2s[:, c, ws, f * P:f * P + P], hsp[:, c % 3, xs, :],
                                          start=c == 0 and e == 0 and chunks != NCS, stop=c == chunks - 1 and e == 2)
                        last.then_inc(s_m2, 1)

                    def transpose_out(blk, f):
                        Y = first_y + blk
                        pe.wait_ge(s_ye, Y + 1 + 1)
                        pe.wait_ge(s_ya, Y * 2 + f + 1)
                        for j in range(2):
                            for k in range(KD):
                                last = tr(ps[:, 7, (j * KD + k) * P:(j * KD + k) * P + P],
                                          ysb[:, k, (2 * f + j) * P:(2 * f + j) * P + P], ident[:, :])
                        last.then_inc(s_yt, 1)

                    def blk_body(blk, lagged, load_w):
                        for c in range(chunks):
                            gate_rows(blk, c)
                            if load_w:
                                pe.wait_ge(s_wl, first_w + c + 1 + 11)
                            hidden(blk, c)
                            if c >= 2:
                                summed(blk, c - 2)
                            elif lagged:
                                summed(blk - 1, chunks - 2 + c)
                            if lagged and c == 2:
                                transpose_out(blk - 1, 0)
                            if lagged and c == min(chunks - 1, 4):
                                transpose_out(blk - 1, 1)
                    blk_body(0, False, True)
                    with pe.Fori(1, NBLK) as blk:
                        blk_body(blk, True, False)
                    summed(NBLK - 1, chunks - 2)
                    summed(NBLK - 1, chunks - 1)
                    transpose_out(NBLK - 1, 0)
                    transpose_out(NBLK - 1, 1)

                with pe.Fori(0, NG) as g:
                    group(g, NCH, L * CHUNKS * NBLK + g * NCH * NBLK, L * (NG + 1) * NBLK + g * NBLK,
                          L * CHUNKS + g * NCH)
                group(NG, NCS, L * CHUNKS * NBLK + NG * NCH * NBLK, L * (NG + 1) * NBLK + NG * NBLK,
                      L * CHUNKS + NG * NCH)
                phase_end(pe, L, 6)


_SHAPES = dict(
    x=(B, T, D), wqkv=(NL, 3, D, D), bqkv=(NL, P, 6), wo=(NL, D, D), bo=(NL, D),
    rw=(D, P), rb=(P, 1), w1=(D, HIDS), w2=(HIDS, D), b1=(P, CHUNKS), b2=(NE + 32, D),
    rows=(NL, 2, SROWS - 48, T), ident=(P, P), masks=(2, P, P), sel=(P, HIDS))


def arrays(i):
    f = np.float32
    i = {k: np.asarray(v) for k, v in i.items()}
    A, Bp, F = "L0_attn_a_", "L0_attn_b_", "L0_ffn_"
    r = {"x": i[A + "x"]}
    r["wqkv"] = np.stack([np.stack([i[A + "k_w"].T, i[A + "q_w"].T, i[A + "v_w"].T]),
                          np.stack([i[Bp + "Wq"], i[Bp + "Wk"], i[Bp + "Wv"]])])
    bias = np.stack([np.stack([i[A + "k_b"], i[A + "q_b"], i[A + "v_b"]]),
                     np.stack([i[Bp + "bq"], i[Bp + "bk"], i[Bp + "bv"]])])
    r["bqkv"] = bias.reshape(NL, 6, P).transpose(0, 2, 1)
    r["wo"] = np.stack([i[A + "o_w"].T, i[Bp + "Wo"]])
    r["bo"] = np.stack([i[A + "o_b"], i[Bp + "bo"]])
    rw = np.zeros((D, P), f)
    rw[:, :NE] = i[F + "router_w"]
    r["rw"] = rw
    rb = np.zeros((P, 1), f)
    rb[:NE, 0] = i[F + "router_b"]
    r["rb"] = rb
    w1 = np.zeros((D, HIDS), f)
    w2 = np.zeros((HIDS, D), f)
    b1 = np.zeros((HIDS,), f)
    n, m = NE * HID, (NE + NSH) * HID
    w1[:, :n] = i[F + "rw1"].transpose(1, 0, 2).reshape(D, n)
    w1[:, n:m] = i[F + "sw1"].transpose(1, 0, 2).reshape(D, m - n)
    w2[:n] = i[F + "rw2"].reshape(n, D)
    w2[n:m] = i[F + "sw2"].reshape(m - n, D)
    b1[:n] = i[F + "rb1"].reshape(n)
    b1[n:m] = i[F + "sb1"].reshape(m - n)
    r["w1"], r["w2"], r["b1"] = w1, w2, b1.reshape(CHUNKS, P).T
    b2 = np.zeros((NE + 32, D), f)
    b2[:NE] = i[F + "rb2"]
    b2[NE:NE + NSH] = i[F + "sb2"]
    r["b2"] = b2
    t = np.arange(T, dtype=f)
    rows = np.zeros((NL, 2, SROWS - 48, T), f)
    rows[0, 0, 16], rows[0, 0, 17] = -t, 1.0
    rows[0, 1, 16], rows[0, 1, 17] = 1.0, t
    rows[:, 1, 18:20] = 1.0
    r["rows"] = rows
    r["ident"] = np.eye(P, dtype=f)
    q, k = np.arange(P)[:, None], np.arange(P)[None, :]
    r["masks"] = np.stack([np.where(k > q, NEG, 0.0), np.where(q > k, NEG, 0.0)]).astype(f)
    sel = np.zeros((P, HIDS), np.float16)
    for e in range(NE + NSH):
        for row in ((e, NE + e, 2 * NE + e) if e < NE else (3 * NE + e - NE,)):
            sel[row, e * HID:(e + 1) * HID] = 1.0
    r["sel"] = sel
    return {k: np.ascontiguousarray(v) for k, v in r.items()}


def kernel(**inputs):
    import concourse.bacc as _bacc
    from concourse.bass_utils import run_bass_kernel_spmd as _run

    nc = _bacc.Bacc("TRN2", target_bir_lowering=False, num_devices=1)
    laid = arrays(inputs)
    aps = {k: nc.dram_tensor(f"in_{k}", shape, F16 if k == "sel" else F32, kind="ExternalInput").ap()
           for k, shape in _SHAPES.items()}
    out = nc.dram_tensor("out_0", (B, T, D), F32, kind="ExternalOutput").ap()
    build(nc, aps, out)
    r = _run(nc, [{f"in_{k}": laid[k] for k in _SHAPES}], core_ids=[0])
    return r.results[0]["out_0"]
```

```python
from contextlib import ExitStack

import numpy as np

import concourse.bass as bass
from concourse import mybir

F32 = mybir.dt.float32
F32R = mybir.dt.float32r
BF16 = mybir.dt.bfloat16
F16 = mybir.dt.float16
ALU = mybir.AluOpType
ACT = mybir.ActivationFunctionType
AX = mybir.AxisListType
ds = bass.ds

P = 128
B, T, D = 4, 1024, 256
H, HD = 16, 16
NL = 2
NTOK = B * T
NT = NTOK // P
BLK = 512
NBLK = NTOK // BLK
TPB = BLK // P
KD = D // P
EPS = 1e-5
NEG = -(2.0 ** 100)

NE, NSH, TOPK, HID = 32, 2, 6, 176
NCH = 11
NG = NE * HID // (NCH * P)
NCS = 3
CHUNKS = NG * NCH + NCS
HIDS = CHUNKS * P
GROUPS = [NCH] * NG + [NCS]

HG = 4
NU = B * H // HG
NQB = T // P
SROWS = 68

NPHASE = 7
ENGINES = 5


def max_jobs():
    jobs = []
    for i in range(NQB):
        first = 0
        if i >= 4:
            jobs += [(i, 0, BLK, [h]) for h in range(HG)]
            first = BLK
        w = (i + 1) * P - first
        per = min(HG, BLK // w)
        jobs += [(i, first, w, list(range(h, min(h + per, HG)))) for h in range(0, HG, per)]
    return jobs


def slot_age(c, chunks, ring):
    if c >= ring:
        return ring
    return c + chunks - max(k for k in range(chunks) if k % ring == c % ring)


def raw_count(L, g, c):
    if isinstance(g, int) and g == NG:
        return 32 * (L * 9 + 9)
    if c < 3:
        return 32 * (L * 9 + g * 2 + 1)
    if c >= 8:
        return 32 * (L * 9 + g * 2 + 2)
    return 32 * (L * 4 + g + 1)


def stack_count(L, turn, r):
    return (L * (6, 5, 5)[r] + turn + 1) * 128


def task_of(j):
    return j if j < OUT0_AT else j + 1


def exp_slots():
    return [(qt, kb, BLK if kb < 4 * qt else BLK - (kb - 4 * qt) * P)
            for qt in range(T // BLK) for kb in range(4 * qt + 4)]


MAX_JOBS = max_jobs()
SLOTS = exp_slots()
NJ, NS = len(MAX_JOBS), len(SLOTS)
WHEAD = 8
MAX_SLOTS = 8
STEP_JOBS = NJ + 2
OUT0_AT = NJ * 7 // MAX_SLOTS
LAYER_JOBS = NJ + (NU - 1) * STEP_JOBS + 2
JOB_BANKS = (4, 5, 7)
STEP_LINKS = 5
CHAIN = 133
PRODUCTS = ((0, 0), (0, 1), (1, 0))
Q_SCALE = HD ** -0.5


def build(nc, a, out):
    qks = nc.dram_tensor("qks_scratch", (2, 2, NU, 64, T), F32, kind="Internal").ap()
    vds = nc.dram_tensor("v_scratch", (NU, P, NQB, HG * 32), F32, kind="Internal").ap()

    rows_scratch = nc.dram_tensor("rows_scratch", (NL, 2, SROWS - 48, T), F32, kind="Internal").ap()

    ctx = ExitStack()
    with ctx:
        def sb(name, shape, dt):
            return ctx.enter_context(nc.sbuf_tensor(name, shape, dt))

        def sem(name):
            return ctx.enter_context(nc.semaphore(name))

        split = sb("split", [P, 30720], F32R)
        xT = split[:, 0:16384].rearrange("p (k s t) -> p k s t", k=KD, s=2)
        wreg = split[:, 16384:27648]
        hsp = split[:, 27648:30720].rearrange("p (r s t) -> p r s t", r=3, s=2)
        stack = split[:, 0:24576].rearrange("p (r o h t) -> p r o h t", r=3, o=2, h=HG)
        stack32 = stack.bitcast(F32)
        vreg = split[:, 24576:27648].bitcast(F32).rearrange("p (r t h c) -> p r t h c", r=3, t=NQB, h=HG)
        wqkv = wreg[:, 0:3072].rearrange("p (m k s n) -> p m k s n", m=3, k=KD, s=2)
        qkst = wreg[:, 3072:11264].rearrange("p (r m s f t) -> p r m s f t", r=2, m=2, s=2, f=2)
        w1s = wreg.rearrange("p (c j) -> p c j", j=1024)[:, :, 0:512].rearrange(
            "p c (k s n) -> p c k s n", k=KD, s=2)
        w2s = wreg.rearrange("p (c j) -> p c j", j=1024)[:, :, 512:1024].rearrange(
            "p c (s n) -> p c s n", s=2)

        x = sb("x", [P, NT * D], F32)
        work = sb("work", [P, 12288], F32)
        attn = work[:, 0:8192].rearrange("p (u t c) -> p u t c", u=NU, t=NQB)
        pexp = work[:, 8192:12288].rearrange("p (r h t) -> p r h t", r=4, h=2)
        xn = work[:, 8192:10240].rearrange("p (r t d) -> p r t d", r=2, t=TPB)
        fqk = work[:, 0:2048].rearrange("p (r f t) -> p r f t", r=2, f=2)
        vst = work[:, 2048:6144].rearrange("p (r t h c) -> p r t h c", r=2, t=TPB, h=H)
        vf = work[:, 6144:8192].rearrange("p (r f t) -> p r f t", r=2, f=2)
        mask32 = work[:, 0:2 * P].rearrange("p (m k) -> p m k", m=2)
        wraw = work[:, 10240:11776].rearrange("p (m k n) -> p m k n", m=3, k=KD)
        mtok = work[:, 8192:10240].rearrange("p (r t d) -> p r t d", r=2, t=TPB)
        mT = work[:, 10240:12288].rearrange("p (r k t) -> p r k t", r=2, k=KD)
        gT = work[:, 0:2048].bitcast(BF16)
        sel = work[:, 2048:2048 + HIDS // 2].bitcast(F16)
        hbuf = work[:, 5120:6656].rearrange("p (r t) -> p r t", r=3)
        ysb = work[:, 6656:7680].rearrange("p (f t) -> p f t", f=KD)
        raw = work[:, 7680:11776].rearrange("p (r n) -> p r n", r=8)
        b2s = work[:, 11776:12160].bitcast(BF16).rearrange("p (s d) -> p s d", s=3)
        lgt = work[:, 5120:6208].rearrange("p (t e) -> p t e", e=NE + 2)
        prb = work[:, 6208:7296].rearrange("p (t e) -> p t e", e=NE + 2)
        rep = work[:, 7296:8384].rearrange("p (t e) -> p t e", e=NE + 2)
        gst = work[:, 8384:10432].bitcast(BF16).rearrange("p (t c) -> p t c", c=P)
        lgT = work[:, 10432:11456].rearrange("p (r t) -> p r t", r=2)
        top = work[:, 11456:11712].rearrange("p (t e) -> p t e", e=8)
        b2f = work[:, 5120:5888].rearrange("p (s d) -> p s d", s=3)

        osb = sb("osb", [P, BLK], F32)
        wo = osb
        stat = work[:, 11776:11968].rearrange("p (t s) -> p t s", s=6)
        sv = work[:, 11968:12288].rearrange("p (s t) -> p s t", s=10)
        small = sb("small", [P, 600], F32)
        mpart = small[:, 0:64].rearrange("p (s c) -> p s c", s=2)
        mneg = small[:, 64:96]
        mtr = small[:, 96:128]
        mhl = sb("mhl", [P, 3, 2, 32], F32R)
        rden = small[:, 176:208].rearrange("p (r c) -> p r c", r=2)
        bqkv = small[:, 208:214]
        bq4 = small[:, 214:216]
        b1 = small[:, 216:216 + CHUNKS]
        rb = small[:, 264:265]
        bo = small[:, 272:528]
        mx8 = small[:, 528:560]
        sm8 = small[:, 560:592]
        ident = sb("ident", [P, P], F32)
        identb = sb("identb", [P, P], BF16)
        maskq = sb("maskq", [P, P], BF16)
        maskk = sb("maskk", [P, P], BF16)

        ps = ctx.enter_context(nc.psum_tensor("ps", [P, 8, BLK], F32))

        s_const, s_x, s_phase = sem("const_loaded"), sem("x_loaded"), sem("phase_done")
        s_apart = sem("wait_carrier")
        s_chain = sem("dve_chain")
        s_var, s_sd = sem("var_ready"), sem("sd_ready")
        s_xn, s_tp, s_xh, s_xl = sem("xn_ready"), sem("xT_psum_ready"), sem("xT_hi_done"), sem("xT_lo_done")
        s_wload, s_wsplit = sem("qkv_weights_loaded"), sem("qkv_weights_split")
        s_pj, s_pf = sem("proj_ready"), sem("proj_evacuated")
        s_ph, s_pl, s_pd = sem("qk_hi_done"), sem("qk_lo_done"), [sem(f"qk_stored{r}") for r in range(2)]
        s_vt, s_vs, s_vd = sem("v_transposed"), sem("v_staged"), [sem(f"v_stored{r}") for r in range(2)]
        s_rows = [sem(f"constant_rows_loaded{r}") for r in range(3)]
        s_zero = [sem(f"stack_zeroed{r}") for r in range(3)]
        s_stk = [sem(f"stack_loaded{r}") for r in range(3)]
        s_st, s_pe, s_pv = sem("scoresT_ready"), sem("exp_done"), sem("values_done")
        s_mj, s_mr = sem("task_ready"), sem("task_done")
        s_mt, s_mrow = sem("neg_max_split"), sem("neg_max_rows_loaded")
        s_ov = sem("out_evacuated")
        s_bo, s_bod = sem("merge_bias_loaded"), sem("merge_bias_added")
        s_mc, s_mtp, s_mev, s_mo, s_ma = (sem("merge_tokens_copied"), sem("merge_transposed"),
                                          sem("merge_evacuated"), sem("merge_product"), sem("merge_added"))
        s_rld, s_rsp = sem("router_loaded"), sem("router_split")
        s_lg, s_lge, s_lgt, s_lgd = (sem("logitsT_ready"), sem("logitsT_evacuated"),
                                     sem("logits_transposed"), sem("logits_stored"))
        s_le, s_ee, s_gs, s_gt, s_gd = (sem("logits_shifted"), sem("logits_exp"), sem("gates_split"),
                                        sem("gates_transposed"), sem("gatesT_stored"))
        s_raw = [sem(f"expert_raw_loaded{r}") for r in range(8)]
        s_wh, s_wl = sem("expert_hi_done"), sem("expert_lo_done")
        s_m2, s_y0 = sem("chunk_summed"), sem("first_half_summed")
        s_g, s_h, s_r, s_hg, s_hi, s_lo = (sem("gate_rows_ready"), sem("hidden_ready"), sem("relu_done"),
                                           sem("gated_done"), sem("hidden_hi_done"), sem("hidden_lo_done"))
        s_ye, s_yt, s_ya = sem("out_copied"), sem("outT_ready"), sem("out_added")
        s_out = sem("result_stored")
        block = ctx.enter_context(nc.Block())

        def apart(e):
            e.sem_inc(s_apart, 1)

        def phase_end(e, L, n):
            apart(e)
            e.drain().then_inc(s_phase, 1)
            e.wait_ge(s_phase, (L * NPHASE + n + 1) * ENGINES)
            apart(e)

        @block.sync
        def _(sp):
            sp.dma_start(ident[:, :], a["ident"]).then_inc(s_const, 16)
            sp.dma_start(mask32, a["masks"].rearrange("m p k -> p m k")).then_inc(s_const, 16)
            sp.dma_start(rows_scratch, a["rows"]).then_inc(s_const, 16)
            xv = x[:, :].rearrange("p (t d) -> p t d", d=D)
            xin = a["x"].rearrange("b (t p) d -> p (b t) d", p=P)
            for q in range(4):
                sp.dma_start(xv[:, 8 * q:8 * q + 8, :], xin[:, 8 * q:8 * q + 8, :]).then_inc(s_x, 16)

            with sp.Fori(0, NL) as L:
                for m in range(3):
                    sp.dma_start(wraw[:, m], a["wqkv"][L, m].rearrange("(k p) n -> p k n", p=P)).then_inc(s_wload, 16)
                sp.dma_start(bqkv, a["bqkv"][L]).then_inc(s_wload, 16)
                sp.dma_start(bo, a["bo"][ds(L, 1)].partition_broadcast(P).rearrange("p o d -> p (o d)")).then_inc(s_bo, 16)
                phase_end(sp, L, 0)
                with sp.Fori(0, B) as b:
                    for r in range(2):
                        n = L * NBLK + b * 2 + r
                        sp.wait_ge(s_pl, n * 4 + 4 + 4)
                        apart(sp)
                        for m in range(2):
                            for s in range(2):
                                sp.dma_start(
                                    qks[m, s, ds(b * HG, HG), :, r * BLK:(r + 1) * BLK]
                                    .rearrange("(f e) w t -> (e w) f t", f=2),
                                    qkst[:, r, m, s].bitcast(F32)).then_inc(s_pd[r], 16)
                        sp.wait_ge(s_vs, n + 1 + 1)
                        for u in range(HG):
                            sp.dma_start(
                                vds[b * HG + u, :, r * TPB:(r + 1) * TPB, :],
                                vst[:, r, :, HG * u:HG * u + HG, :].rearrange("p t h c -> p t (h c)")
                            ).then_inc(s_vd[r], 16)
                for r in range(2):
                    sp.wait_ge(s_pd[r], (L * B + B) * 64 + 64)
                    sp.wait_ge(s_vd[r], (L * B + B) * 64 + 64)
                phase_end(sp, L, 1)

                sp.wait_ge(s_const, 48)
                def load_unit(u, r, again=True):
                    if again:
                        sp.wait_ge(s_pv, (L * NU + u - 2) * NS + 2)
                    for o in range(2):
                        for g, s in enumerate(((0, 0, 1), (0, 1, 0))[o]):
                            sp.dma_start(stack32[16 * g:16 * g + 16, r, o],
                                         qks[o, s, u].rearrange("(h w) t -> w h t", h=HG)).then_inc(s_stk[r], 16)
                    sp.dma_start(vreg[:, r], vds[u].rearrange("p t (h c) -> p t h c", h=HG)).then_inc(s_stk[r], 16)
                    sp.wait_ge(s_rows[r], (L + 1) * 32)
                    sp.dma_start(stack32[66:68, r, 0], rows_scratch[L, 0, 0:2].unsqueeze(1)
                                 .broadcast_to([2, HG, T])).then_inc(s_stk[r], 16)

                for r in range(3):
                    sp.wait_ge(s_zero[r], (L + 1) * 2)
                    for o in range(2):
                        sp.dma_start(stack32[48:SROWS, r, o], rows_scratch[L, o].unsqueeze(1)
                                     .broadcast_to([SROWS - 48, HG, T])).then_inc(s_rows[r], 16)
                    load_unit(r, r, again=False)
                def load_neg_max(u, r):
                    sp.wait_ge(s_mt, L * NU + u + 1)
                    for s in range(2):
                        for q in range(4):
                            row = stack32[66 + s:67 + s, r, 0].rearrange("p h t -> p (h t)")
                            row = row.rearrange("p (c q w) -> p q c w", q=4, w=32)[:, q]
                            sp.dma_start(row, mhl[32 * q:32 * q + 32, r, s, :].bitcast(F32)).then_inc(s_mrow, 16)

                load_neg_max(0, 0)
                with sp.Fori(0, 4) as i:
                    for r in range(3):
                        load_neg_max(i * 3 + r + 1, (r + 1) % 3)
                        load_unit(i * 3 + r + 3, r)
                load_neg_max(13, 1)
                load_unit(15, 0)
                load_neg_max(14, 2)
                load_neg_max(15, 0)
                phase_end(sp, L, 2)
                sp.dma_start(wo[:, :].rearrange("p (k n) -> p k n", k=KD),
                             a["wo"][L].rearrange("(k p) n -> p k n", p=P)).then_inc(s_bo, 16)
                phase_end(sp, L, 3)

                sp.dma_start(raw[:, 0, 0:256].rearrange("p (k n) -> p k n", k=KD),
                             a["rw"].rearrange("(k p) n -> p k n", p=P)).then_inc(s_rld, 16)
                sp.dma_start(rb, a["rb"]).then_inc(s_rld, 16)
                sp.dma_start(b1, a["b1"]).then_inc(s_rld, 16)
                sp.dma_start(sel, a["sel"]).then_inc(s_rld, 16)
                phase_end(sp, L, 4)
                sp.wait_ge(s_gs, (L + 1) * 1)
                for s in range(3):
                    sp.dma_start(b2f[32 * s:32 * s + 32, 0, :], a["b2"][0:NE]).then_inc(s_rld, 16)
                sp.dma_start(b2f[96:128, 0, :], a["b2"][NE:NE + 32]).then_inc(s_rld, 16)
                phase_end(sp, L, 5)

                def load_chunk(col, c, n):
                    r = c % 8
                    sp.wait_ge(s_wl, n)
                    sp.dma_start(raw[:, r, 0:256].rearrange("p (k n) -> p k n", k=KD),
                                 a["w1"][:, ds(col, P)].rearrange("(k p) n -> p k n", p=P)).then_inc(s_raw[r], 16)
                    sp.dma_start(raw[:, r, 256:512], a["w2"][ds(col, P), :]).then_inc(s_raw[r], 16)

                with sp.Fori(0, NG) as g:
                    for c in range(NCH):
                        n = L * CHUNKS + g * NCH + c
                        n = n - 8 if c >= 8 else (n + 8 - NCH if c + 8 < NCH else n - NCH)
                        load_chunk((g * NCH + c) * P, c, n + 1 + 11)
                for c in range(NCS):
                    load_chunk((NG * NCH + c) * P, c, L * CHUNKS + NG * NCH + c + 8 - NCH + 1 + 11)
                phase_end(sp, L, 6)

            xo = out.rearrange("b (t p) d -> p (b t) d", p=P)
            for q in range(4):
                sp.dma_start(xo[:, 8 * q:8 * q + 8, :], xv[:, 8 * q:8 * q + 8, :]).then_inc(s_out, 16)
            sp.wait_ge(s_out, 64)

        @block.vector
        def _(dve):
            v = nc.vector
            dve.sem_inc(s_xl, 2)
            dve.sem_inc(s_vs, 1)
            dve.sem_inc(s_mr, 3)
            dve.sem_inc(s_ma, 2)
            dve.sem_inc(s_lgd, 2)
            dve.sem_inc(s_gd, 2)
            dve.sem_inc(s_hg, 2)
            dve.sem_inc(s_ya, 1)
            chain = [0]
            turns = [0]

            def link(ins):
                chain[0] += 1
                ins.then_inc(s_chain, 1)

            dve.wait_ge(s_const, 48)
            v.tensor_copy(identb[:, :], ident[:, :])
            v.tensor_copy(maskq[:, :], mask32[:, 0, :])
            v.tensor_copy(maskk[:, :], mask32[:, 1, :])
            dve.wait_ge(s_x, 64)

            with dve.Fori(0, NL) as L:
                chain[0] = 0

                def linked():
                    dve.wait_ge(s_chain, L * CHAIN + turns[0] + chain[0])

                def norm(k):
                    with dve.Fori(0, NT // 4) as t:
                        for j in range(4):
                            last = v.bn_stats(stat[:, ds(t * 4 + j, 1), :].rearrange("p t s -> p (t s)"),
                                              x[:, ds((t * 4 + j) * D, D)])
                        last.then_inc(s_chain, 1)
                    chain[0] += NT // 4
                    linked()
                    me, ve, mo, vo = (stat[:, :, s] for s in (1, 2, 4, 5))
                    v.tensor_tensor(sv[:, 0], me, mo, ALU.subtract)
                    v.tensor_tensor(sv[:, 1], me, mo, ALU.add)
                    link(v.tensor_tensor(sv[:, 2], ve, vo, ALU.add))
                    linked()
                    v.tensor_tensor(sv[:, 3], sv[:, 0], sv[:, 0], ALU.mult)
                    link(v.tensor_scalar(sv[:, 4], sv[:, 2], 1.0 / D, EPS, ALU.mult, ALU.add))
                    linked()
                    v.scalar_tensor_tensor(sv[:, 5], sv[:, 3], 0.25, sv[:, 4], ALU.mult, ALU.add).then_inc(s_var, 1)
                    dve.wait_ge(s_sd, k + 1)
                    link(v.reciprocal(sv[:, 7], sv[:, 6]))
                    linked()
                    link(v.tensor_tensor(sv[:, 7], sv[:, 5], sv[:, 7], ALU.mult))
                    linked()
                    link(v.tensor_tensor(sv[:, 7], sv[:, 6], sv[:, 7], ALU.add))
                    linked()
                    link(v.reciprocal(sv[:, 7], sv[:, 7]))
                    linked()
                    link(v.tensor_scalar(sv[:, 8], sv[:, 7], 2.0, None, ALU.mult))
                    linked()
                    link(v.scalar_tensor_tensor(sv[:, 9], sv[:, 1], -0.5, sv[:, 8], ALU.mult, ALU.mult))
                    linked()
                    apart(dve)
                    with dve.Fori(0, NBLK // 2) as i:
                        for r in range(2):
                            n = k * NBLK + i * 2 + r
                            dve.wait_ge(s_tp, n + 1)
                            for j in range(TPB):
                                t = (i * 2 + r) * TPB + j
                                last = v.tensor_scalar(xn[:, r, j, :], x[:, ds(t * D, D)], sv[:, 8, ds(t, 1)],
                                                       sv[:, 9, ds(t, 1)], ALU.mult, ALU.add)
                            last.then_inc(s_xn, 1)
                        for r in range(2):
                            n = k * NBLK + i * 2 + r
                            dve.wait_ge(s_xh, n + 1)
                            col = ds((i * 2 + r) * BLK, BLK)
                            v.tensor_tensor(xT[:, :, 1, col], ps[:, 2 * r:2 * r + 2, :],
                                            xT[:, :, 0, col].bitcast(F32), ALU.subtract).then_inc(s_xl, 1)

                norm(L * 2)
                phase_end(dve, L, 0)

                dve.wait_ge(s_wload, (L + 1) * 64)
                v.tensor_scalar(bq4, bqkv[:, 0:2], HD ** -0.5, None, ALU.mult)
                link(v.tensor_copy(wqkv[:, :, :, 0, :], wraw))
                linked()
                v.tensor_tensor(wqkv[:, :, :, 1, :], wraw, wqkv[:, :, :, 0, :].bitcast(F32),
                                ALU.subtract).then_inc(s_wsplit, 1)
                v.memset(vst[:, :, :, :, HD:32], 1.0)
                with dve.Fori(0, B) as b:
                    for r in range(2):
                        n = L * NBLK + b * 2 + r
                        dve.wait_ge(s_pd[r], (L * B + b) * 64 + 64)
                        for m in range(2):
                            for f in range(2):
                                dve.wait_ge(s_pf, n * 6 + m * 2 + f + 1 + 3)
                                v.tensor_copy(qkst[:, r, m, 0, f], fqk[:, m, f]).then_inc(s_ph, 1)
                        dve.wait_ge(s_vd[r], (L * B + b) * 64 + 64)
                        dve.wait_ge(s_vt, n + 1 + 2)
                        for f in range(2):
                            last = v.tensor_copy(vst[:, r, :, 8 * f:8 * f + 8, 0:HD],
                                                 ps[:, 6 + f, :].rearrange("p (t h c) -> p t h c", t=TPB, h=8))
                        last.then_inc(s_vs, 1)
                phase_end(dve, L, 1)

                v.memset(stack32[64:P, 0, 0], 0.0).then_inc(s_zero[0], 1)

                def base(u):
                    return L * LAYER_JOBS + NJ + u * STEP_JOBS

                def max_job(task, ring, j):
                    i, first, w, heads = MAX_JOBS[j]
                    dve.wait_ge(s_mj, task + 1)
                    cols = mpart[:, 0 if first or i < 4 else 1, :].rearrange("p (h q) -> p h q", h=HG)
                    v.tensor_reduce(cols[:, heads[0]:heads[0] + len(heads), i],
                                    ps[:, JOB_BANKS[ring % 3], 0:w * len(heads)].rearrange("p (h k) -> p h k", k=w),
                                    AX.X, ALU.max, negate=True).then_inc(s_mr, 1)

                def split_max(r, tasks):
                    late = mpart[:, :, :].rearrange("p s (h q) -> p s h q", h=HG)
                    neg = mneg.rearrange("p (h q) -> p h q", h=HG)
                    dve.wait_ge(s_mr, tasks + 3)
                    v.tensor_copy(neg[:, :, 0:4], late[:, 0, :, 0:4])
                    link(v.tensor_tensor(neg[:, :, 4:8], late[:, 0, :, 4:8], late[:, 1, :, 4:8], ALU.min))
                    linked()
                    link(v.transpose(mtr, mneg))
                    linked()
                    link(v.tensor_copy(mhl[:, r, 0, :], mtr))
                    linked()
                    v.tensor_tensor(mhl[:, r, 1, :], mtr, mhl[:, r, 0, :].bitcast(F32),
                                    ALU.subtract).then_inc(s_mt, 1)

                def normalise(u, qt, task, ring):
                    dve.wait_ge(s_mj, task + 1)
                    o = ps[:, JOB_BANKS[ring % 3], :].rearrange("p (q h c) -> p q h c", q=4, h=HG)
                    rd = rden[:, qt].rearrange("p (q h) -> p q h", q=4)
                    link(v.reciprocal(rd, o[:, :, :, HD]))
                    linked()
                    v.tensor_tensor(
                        attn[:, ds(u, 1), 4 * qt:4 * qt + 4, :].rearrange("p u t (h c) -> p (u t h) c", h=HG),
                        o[:, :, :, 0:HD].rearrange("p q h c -> p (q h) c"),
                        rden[:, qt].unsqueeze(2).broadcast_to([P, 16, HD]), ALU.mult).then_inc(s_mr, 1)

                def step(u, r):
                    ring = r * STEP_JOBS
                    for j in range(NJ):
                        if j == OUT0_AT:
                            normalise(u, 0, base(u) + j, ring + j)
                        max_job(base(u) + task_of(j), ring + task_of(j), j)
                    split_max((r + 1) % 3, base(u) + NJ + 1)
                    normalise(u, 1, base(u) + NJ + 1, ring + NJ + 1)

                for j in range(NJ):
                    max_job(L * LAYER_JOBS + j, j + 1, j)
                split_max(0, L * LAYER_JOBS + NJ)
                with dve.Fori(0, 5) as i:
                    before = chain[0]
                    turns[0] = i * (3 * STEP_LINKS)
                    for r in range(3):
                        step(i * 3 + r, r)
                    turns[0] = 0
                    assert chain[0] == before + 3 * STEP_LINKS
                chain[0] += 4 * 3 * STEP_LINKS
                for qt in range(2):
                    normalise(NU - 1, qt, base(NU - 1) + qt, qt)
                phase_end(dve, L, 2)

                with dve.Fori(0, NBLK // 2) as i:
                    for r in range(2):
                        n = L * NBLK + i * 2 + r
                        dve.wait_ge(s_mtp, n + 1)
                        for g in range(HG):
                            last = v.tensor_copy(mtok[:, r, :, 64 * g:64 * g + 64],
                                                 attn[:, ds((i * HG) + g, 1), TPB * r:TPB * r + TPB, :]
                                                 .rearrange("p u t c -> p (u t) c"))
                        last.then_inc(s_mc, 1)
                    for r in range(2):
                        n = L * NBLK + i * 2 + r
                        dve.wait_ge(s_mo, n + 1 + 2)
                        if r == 0:
                            dve.wait_ge(s_bod, (L + 1) * NT)
                        xb = x[:, ds((i * 2 + r) * TPB * D, TPB * D)]
                        v.tensor_tensor(xb, ps[:, 4 + 2 * r:6 + 2 * r, :].rearrange("p f t -> p (f t)"), xb,
                                        ALU.add).then_inc(s_ma, 1)
                phase_end(dve, L, 3)
                norm(L * 2 + 1)
                dve.wait_ge(s_rld, L * 128 + 64)
                link(v.tensor_copy(hsp[:, 0, 0, 0:256], raw[:, 0, 0:256]))
                linked()
                v.tensor_tensor(hsp[:, 0, 1, 0:256], raw[:, 0, 0:256], hsp[:, 0, 0, 0:256].bitcast(F32), ALU.subtract)
                phase_end(dve, L, 4)

                with dve.Fori(0, NBLK // 2) as i:
                    for r in range(2):
                        n = L * NBLK + i * 2 + r
                        dve.wait_ge(s_lgt, n + 1 + 2)
                        v.tensor_copy(lgt[:, ds((i * 2 + r) * TPB, TPB), 0:NE],
                                      ps[:, 2 + r, 0:TPB * NE].rearrange("p (t e) -> p t e", e=NE)).then_inc(s_lgd, 1)
                dve.wait_ge(s_lgd, (L + 1) * NBLK + 2)
                link(v.tensor_reduce(mx8, lgt[:, :, 0:NE], AX.X, ALU.max))
                linked()
                v.tensor_tensor(lgt[:, :, 0:NE], lgt[:, :, 0:NE], mx8.unsqueeze(2).broadcast_to([P, NT, NE]),
                                ALU.subtract).then_inc(s_le, 1)
                dve.wait_ge(s_ee, L + 1)
                v.memset(prb[:, :, NE:NE + 2], -1.0)
                link(v.tensor_reduce(sm8, rep[:, :, 0:NE], AX.X, ALU.add))
                linked()
                link(v.reciprocal(sm8, sm8))
                linked()
                link(v.tensor_tensor(prb[:, :, 0:NE], rep[:, :, 0:NE], sm8.unsqueeze(2).broadcast_to([P, NT, NE]),
                                     ALU.mult))
                linked()
                apart(dve)
                for t in range(NT):
                    last = v.max(top[:, t, :], prb[:, t, :])
                link(last)
                linked()
                link(v.memset(top[:, :, TOPK:8], -1.0))
                linked()
                apart(dve)
                for t in range(NT):
                    last = v.match_replace(rep[:, t, :], top[:, t, :], prb[:, t, :], 0.0)
                link(last)
                linked()
                g = lgt[:, :, 0:NE]
                link(v.tensor_tensor(g, prb[:, :, 0:NE], rep[:, :, 0:NE], ALU.subtract))
                linked()
                link(v.tensor_reduce(sm8, g, AX.X, ALU.add))
                linked()
                link(v.reciprocal(sm8, sm8))
                linked()
                link(v.tensor_tensor(g, g, sm8.unsqueeze(2).broadcast_to([P, NT, NE]), ALU.mult))
                linked()
                v.memset(gst[:, :, 3 * NE:P], 0.0)
                link(v.tensor_copy(gst[:, :, 0:NE], g))
                linked()
                v.memset(gst[:, :, 3 * NE:3 * NE + NSH], 1.0 / NSH)
                link(v.tensor_tensor(g, g, gst[:, :, 0:NE], ALU.subtract))
                linked()
                link(v.tensor_copy(gst[:, :, NE:2 * NE], g))
                linked()
                link(v.tensor_tensor(g, g, gst[:, :, NE:2 * NE], ALU.subtract))
                linked()
                v.tensor_copy(gst[:, :, 2 * NE:3 * NE], g).then_inc(s_gs, 1)
                for n in range(NBLK):
                    dve.wait_ge(s_gt, L * NBLK + n + 1)
                    v.tensor_copy(gT[:, n * BLK:(n + 1) * BLK],
                                  ps[:, n % 2, 0:BLK // 2].bitcast(BF16)).then_inc(s_gd, 1)
                dve.wait_ge(s_rld, L * 128 + 128)
                link(v.tensor_copy(b2s[:, 0, :], b2f[:, 0, :]))
                linked()
                link(v.tensor_tensor(b2f[:, 1, :], b2f[:, 0, :], b2s[:, 0, :], ALU.subtract))
                linked()
                link(v.tensor_copy(b2s[:, 1, :], b2f[:, 1, :]))
                linked()
                link(v.tensor_tensor(b2f[:, 2, :], b2f[:, 1, :], b2s[:, 1, :], ALU.subtract))
                linked()
                v.tensor_copy(b2s[:, 2, :], b2f[:, 2, :])
                phase_end(dve, L, 5)

                def gate_mul(n, c):
                    dve.wait_ge(s_r, n + c + 1 + 3)
                    dve.wait_ge(s_g, n + c + 1)
                    v.tensor_tensor(hbuf[:, c % 3, :], ps[:, 3 + c % 2, :], hbuf[:, c % 3, :],
                                    ALU.mult).then_inc(s_hg, 1)

                def hidden_hi(n, c, chunks):
                    dve.wait_ge(s_hg, n + c + 1 + 2)
                    dve.wait_ge(s_m2, n + c + 4 - slot_age(c, chunks, 3))
                    v.tensor_copy(hsp[:, c % 3, 0, :], hbuf[:, c % 3, :]).then_inc(s_hi, 1)

                def out_add(yn, blk, f):
                    dve.wait_ge(s_yt, yn * 2 + f + 1 + 1)
                    xb = x[:, ds(blk * TPB * D + f * 512, 512)]
                    v.tensor_tensor(xb, ps[:, 7, :], xb, ALU.add).then_inc(s_ya, 1)

                def weights_hi(g, c):
                    dve.wait_ge(s_raw[c % 8], raw_count(L, g, c))
                    v.tensor_copy(w1s[:, c, :, 0, :], raw[:, c % 8, 0:256].rearrange("p (k n) -> p k n", k=KD))
                    v.tensor_copy(w2s[:, c, 0, :], raw[:, c % 8, 256:512]).then_inc(s_wh, 1)

                def group(g, chunks, following):
                    first_n, first_y = (L * CHUNKS + g * NCH) * NBLK, (L * (NG + 1) + g) * NBLK

                    def blk_body(blk, first=False, last=False):
                        n = first_n + blk * chunks
                        for c in range(chunks):
                            if first and WHEAD + c < chunks:
                                dve.wait_ge(s_m2, first_n + WHEAD + c - NCH + 4)
                                weights_hi(g, WHEAD + c)
                            gate_mul(n, c)
                            hidden_hi(n, c, chunks)
                            if last and 0 <= c - 3 < min(WHEAD, following):
                                dve.wait_ge(s_m2, n + c - 3 + 4)
                                weights_hi(g + 1, c - 3)
                            if not first and c == 2:
                                out_add(first_y + blk - 1, blk - 1, 0)
                            if not first and c == min(chunks - 1, 4):
                                out_add(first_y + blk - 1, blk - 1, 1)
                    blk_body(0, first=True)
                    with dve.Fori(1, NBLK - 1) as blk:
                        blk_body(blk)
                    blk_body(NBLK - 1, last=True)
                    out_add(first_y + NBLK - 1, NBLK - 1, 0)
                    out_add(first_y + NBLK - 1, NBLK - 1, 1)

                for c in range(WHEAD):
                    weights_hi(0, c)
                with dve.Fori(0, NG - 1) as g:
                    group(g, NCH, NCH)
                group(NG - 1, NCH, NCS)
                group(NG, NCS, 0)
                phase_end(dve, L, 6)
            assert chain[0] == CHAIN, chain[0]

        @block.scalar
        def _(act):
            c = nc.scalar
            act.sem_inc(s_pf, 3)
            act.sem_inc(s_pe, 2)
            act.sem_inc(s_ov, 1)
            act.sem_inc(s_mev, 2)
            act.sem_inc(s_lge, 2)
            act.sem_inc(s_r, 3)
            act.sem_inc(s_ye, KD)
            with act.Fori(0, NL) as L:
                def norm(k):
                    act.wait_ge(s_var, k + 1)
                    c.activation(sv[:, 6], sv[:, 5], ACT.Sqrt).then_inc(s_sd, 1)
                    with act.Fori(0, NBLK // 2) as i:
                        for r in range(2):
                            act.wait_ge(s_tp, k * NBLK + i * 2 + r + 1 + 2)
                            c.activation(xT[:, :, 0, ds((i * 2 + r) * BLK, BLK)], ps[:, 2 * r:2 * r + 2, :],
                                         ACT.Copy).then_inc(s_xh, 1)

                norm(L * 2)
                phase_end(act, L, 0)

                act.wait_ge(s_wsplit, L + 1)
                with act.Fori(0, B) as b:
                    for r in range(2):
                        n = L * NBLK + b * 2 + r
                        for m in range(3):
                            for f in range(2):
                                j = m * 2 + f
                                act.wait_ge(s_pj, n * 6 + j + 1)
                                if m < 2:
                                    act.wait_ge(s_pl, n * 4 + j + 1)
                                elif f == 0:
                                    act.wait_ge(s_vt, n + 1)
                                c.activation(fqk[:, m, f] if m < 2 else vf[:, r, f], ps[:, j % 3, :], ACT.Identity,
                                             bias=bq4[:, f:f + 1] if m == 0 else bqkv[:, j:j + 1],
                                             scale=Q_SCALE if m == 0 else 1.0).then_inc(s_pf, 1)
                phase_end(act, L, 1)

                def evacuate(U, qt, tasks):
                    act.wait_ge(s_pv, U * NS + (4, NS)[qt] + 2)
                    act.wait_ge(s_mj, tasks)
                    c.activation(osb[:, :], ps[:, 6, :], ACT.Copy).then_inc(s_ov, 1)

                def step(u, out0_at):
                    U = L * NU + u
                    base = L * LAYER_JOBS + NJ + u * STEP_JOBS
                    for s, (qt, kb, w) in enumerate(SLOTS):
                        act.wait_ge(s_pv, U * NS + s + 1)
                        for h in range(2):
                            act.wait_ge(s_st, (U * NS + s) * 2 + h + 1)
                            c.activation(pexp[:, (s % 2) * 2 + h, :, BLK - w:], ps[:, 2 * h:2 * h + 2, BLK - w:],
                                         ACT.Exp).then_inc(s_pe, 1)
                        if s == 4:
                            evacuate(U, 0, base)
                    evacuate(U, 1, base + out0_at + 1)

                with act.Fori(0, NU - 1) as u:
                    step(u, OUT0_AT)
                step(NU - 1, 0)
                phase_end(act, L, 2)

                with act.Fori(0, NBLK // 2) as i:
                    for r in range(2):
                        n = L * NBLK + i * 2 + r
                        act.wait_ge(s_mtp, n + 1 + 2)
                        act.wait_ge(s_mo, n + 1)
                        c.activation(mT[:, r], ps[:, 2 * r:2 * r + 2, :], ACT.Copy).then_inc(s_mev, 1)
                phase_end(act, L, 3)
                norm(L * 2 + 1)
                phase_end(act, L, 4)

                act.wait_ge(s_rld, L * 128 + 64)
                with act.Fori(0, NBLK // 2) as i:
                    for r in range(2):
                        n = L * NBLK + i * 2 + r
                        act.wait_ge(s_lg, n + 1)
                        act.wait_ge(s_lgt, n + 1)
                        c.activation(lgT[0:NE, r, :], ps[0:NE, r, :], ACT.Identity,
                                     bias=rb[0:NE, :]).then_inc(s_lge, 1)
                act.wait_ge(s_le, L + 1)
                c.activation(rep[:, :, 0:NE], lgt[:, :, 0:NE], ACT.Exp).then_inc(s_ee, 1)
                phase_end(act, L, 5)

                def group(g, chunks, first_n, first_y):
                    def copy_out(blk):
                        Y = first_y + blk
                        act.wait_ge(s_yt, Y * 2 + 1)
                        for f in range(KD):
                            if f == 0:
                                act.wait_ge(s_y0, Y + 1)
                            else:
                                act.wait_ge(s_m2, first_n + blk * chunks + chunks + 3)
                            c.activation(ysb[:, f], ps[:, 5 + f, :], ACT.Copy).then_inc(s_ye, 1)

                    def blk_body(blk, lagged):
                        for k in range(chunks):
                            Q = first_n + blk * chunks + k
                            act.wait_ge(s_h, Q + 1)
                            act.wait_ge(s_lo, Q + 4 - slot_age(k, chunks, 3))
                            apart(act)
                            c.activation(hbuf[:, k % 3, :], ps[:, k % 3, :], ACT.Relu,
                                         bias=b1[:, ds(g * NCH + k, 1)]).then_inc(s_r, 1)
                            if lagged and k == 1:
                                copy_out(blk - 1)
                    blk_body(0, False)
                    with act.Fori(1, NBLK) as blk:
                        blk_body(blk, True)
                    copy_out(NBLK - 1)

                with act.Fori(0, NG) as g:
                    group(g, NCH, L * CHUNKS * NBLK + g * NCH * NBLK, L * (NG + 1) * NBLK + g * NBLK)
                group(NG, NCS, L * CHUNKS * NBLK + NG * NCH * NBLK, L * (NG + 1) * NBLK + NG * NBLK)
                phase_end(act, L, 6)

        @block.gpsimd
        def _(pool):
            p = nc.gpsimd
            pool.sem_inc(s_pl, 4)
            pool.sem_inc(s_wl, 11)
            pool.sem_inc(s_lo, 3)
            for r in range(2):
                pool.sem_inc(s_pd[r], 64)
                pool.sem_inc(s_vd[r], 64)
            with pool.Fori(0, NL) as L:
                phase_end(pool, L, 0)
                with pool.Fori(0, B) as b:
                    for r in range(2):
                        for m in range(2):
                            for f in range(2):
                                pool.wait_ge(s_ph, (L * NBLK + b * 2 + r) * 4 + m * 2 + f + 1)
                                p.tensor_tensor(qkst[:, r, m, 1, f], fqk[:, m, f], qkst[:, r, m, 0, f].bitcast(F32),
                                                ALU.subtract).then_inc(s_pl, 1)
                phase_end(pool, L, 1)
                p.memset(stack32[64:P, 0, 1], 0.0).then_inc(s_zero[0], 1)
                for r in (1, 2):
                    for o in range(2):
                        p.memset(stack32[64:P, r, o], 0.0).then_inc(s_zero[r], 1)
                pool.wait_ge(s_bo, L * 32 + 16)
                pool.wait_ge(s_zero[2], (L + 1) * 2)
                apart(pool)
                with pool.Fori(0, NT) as t:
                    xt = x[:, ds(t * D, D)]
                    p.tensor_tensor(xt, xt, bo, ALU.add).then_inc(s_bod, 1)
                phase_end(pool, L, 2)
                phase_end(pool, L, 3)
                phase_end(pool, L, 4)
                phase_end(pool, L, 5)

                def weights_lo(g, c):
                    pool.wait_ge(s_wh, L * CHUNKS + g * NCH + c + 1)
                    p.tensor_tensor(w1s[:, c, :, 1, :], raw[:, c % 8, 0:256].rearrange("p (k n) -> p k n", k=KD),
                                    w1s[:, c, :, 0, :].bitcast(F32), ALU.subtract)
                    p.tensor_tensor(w2s[:, c, 1, :], raw[:, c % 8, 256:512], w2s[:, c, 0, :].bitcast(F32),
                                    ALU.subtract).then_inc(s_wl, 1)

                def group(g, chunks, following):
                    first_n = (L * CHUNKS + g * NCH) * NBLK

                    def blk_body(blk, first=False, last=False):
                        for c in range(chunks):
                            if first and WHEAD + c < chunks:
                                weights_lo(g, WHEAD + c)
                            pool.wait_ge(s_hi, first_n + blk * chunks + c + 1)
                            p.tensor_tensor(hsp[:, c % 3, 1, :], hbuf[:, c % 3, :], hsp[:, c % 3, 0, :].bitcast(F32),
                                            ALU.subtract).then_inc(s_lo, 1)
                            if last and 0 <= c - 3 < min(WHEAD, following):
                                weights_lo(g + 1, c - 3)
                    blk_body(0, first=True)
                    with pool.Fori(1, NBLK - 1) as blk:
                        blk_body(blk)
                    blk_body(NBLK - 1, last=True)

                for c in range(WHEAD):
                    weights_lo(0, c)
                with pool.Fori(0, NG - 1) as g:
                    group(g, NCH, NCH)
                group(NG - 1, NCH, NCS)
                group(NG, NCS, 0)
                phase_end(pool, L, 6)

        @block.tensor
        def _(pe):
            mm, tr = nc.tensor.matmul, nc.tensor.transpose
            pe.sem_inc(s_tp, 2)
            pe.sem_inc(s_vt, 2)
            pe.sem_inc(s_pv, 2)
            pe.sem_inc(s_mtp, 2)
            pe.sem_inc(s_mo, 2)
            pe.sem_inc(s_lgt, 2)
            pe.sem_inc(s_m2, 3)
            pe.sem_inc(s_yt, 1)
            pe.wait_ge(s_const, 48)
            with pe.Fori(0, NL) as L:
                def norm(k):
                    with pe.Fori(0, NBLK // 2) as i:
                        for r in range(2):
                            n = k * NBLK + i * 2 + r
                            pe.wait_ge(s_xn, n + 1)
                            pe.wait_ge(s_xl, n + 1)
                            for f in range(KD):
                                for j in range(TPB):
                                    last = tr(ps[:, 2 * r + f, j * P:j * P + P], xn[:, r, j, f * P:f * P + P],
                                              ident[:, :])
                            last.then_inc(s_tp, 1)

                norm(L * 2)
                phase_end(pe, L, 0)

                pe.wait_ge(s_wsplit, L + 1)
                apart(pe)
                with pe.Fori(0, B) as b:
                    for r in range(2):
                        n = L * NBLK + b * 2 + r
                        col = ds((b * 2 + r) * BLK, BLK)
                        for m in range(3):
                            for f in range(2):
                                j = m * 2 + f
                                pe.wait_ge(s_pf, n * 6 + j + 1)
                                for e, (ws, xs) in enumerate(PRODUCTS):
                                    for k in range(KD):
                                        last = mm(ps[:, j % 3, :], wqkv[:, m, k, ws, f * P:f * P + P],
                                                  xT[:, k, xs, col], start=e == 0 and k == 0,
                                                  stop=e == 2 and k == KD - 1)
                                last.then_inc(s_pj, 1)
                        pe.wait_ge(s_pf, n * 6 + 6 + 3)
                        pe.wait_ge(s_vs, n + 1)
                        for f in range(2):
                            for j in range(TPB):
                                last = tr(ps[:, 6 + f, j * P:j * P + P], vf[:, r, f, j * P:j * P + P], ident[:, :])
                        last.then_inc(s_vt, 1)
                phase_end(pe, L, 1)

                def base(u):
                    return L * LAYER_JOBS + NJ + u * STEP_JOBS

                def max_job(task, ring, r, j):
                    i, first, w, heads = MAX_JOBS[j]
                    bank = ps[:, JOB_BANKS[ring % 3], 0:w * len(heads)].rearrange("p (h k) -> p h k", k=w)
                    diagonal = first + w == (i + 1) * P
                    pe.wait_ge(s_mr, task + 1)
                    for e, h in enumerate(heads):
                        last = mm(bank[:, e, :], stack[:, r, 0, h, i * P:i * P + P],
                                  stack[:, r, 1, h, first:first + w], start=e == 0,
                                  stop=not diagonal and e == len(heads) - 1, skip_group_check=True)
                    if diagonal:
                        last = mm(bank[:, :, w - P:w], identb[:, :],
                                  maskq[:, :].unsqueeze(1).broadcast_to([P, len(heads), P]),
                                  start=False, stop=True, skip_group_check=True)
                    last.then_inc(s_mj, 1)

                def scores(U, r, s, half):
                    qt, kb, w = SLOTS[s]
                    pe.wait_ge(s_pe, (U * NS + s) * 2 + half + 1)
                    for e in range(2):
                        h = 2 * half + e
                        last = mm(ps[:, h, BLK - w:], stack[:, r, 1, h, kb * P:kb * P + P],
                                  stack[:, r, 0, h, (qt + 1) * BLK - w:(qt + 1) * BLK],
                                  start=True, stop=kb < 4 * qt, skip_group_check=True)
                        if kb >= 4 * qt:
                            last = mm(ps[:, h, BLK - w:BLK - w + P], identb[:, :], maskk[:, :], start=False, stop=True,
                                      skip_group_check=True)
                    last.then_inc(s_st, 1)

                def values(U, r, s):
                    qt, kb, w = SLOTS[s]
                    if kb == 0:
                        pe.wait_ge(s_ov, U * 2 + qt + 1)
                    pe.wait_ge(s_pe, (U * NS + s) * 2 + 2 + 2)
                    for h in range(HG):
                        last = mm(ps[32 * h:32 * h + 32, 6, BLK - w:], vreg[:, r, kb, h, :],
                                  pexp[:, (s % 2) * 2 + h // 2, h % 2, BLK - w:], start=kb == 0,
                                  stop=kb == 4 * qt + 3, skip_group_check=True)
                    last.then_inc(s_pv, 1)

                def transpose_out(U, qt, task, ring):
                    pe.wait_ge(s_ov, U * 2 + qt + 1 + 1)
                    pe.wait_ge(s_mr, task + 1)
                    for j in range(4):
                        last = tr(ps[:, JOB_BANKS[ring % 3], j * P:j * P + P], osb[:, j * P:j * P + P], ident[:, :])
                    last.then_inc(s_mj, 1)

                def first_scores(U, r):
                    pe.wait_ge(s_mrow, (U + 1) * 128)
                    for half in range(2):
                        scores(U, r, 0, half)

                def step(turn, r, ahead=True):
                    u = turn * 3 + r
                    U = L * NU + u
                    ring = r * STEP_JOBS
                    job = 0
                    if ahead:
                        pe.wait_ge(s_stk[(r + 1) % 3], stack_count(L, turn + (r + 1) // 3, (r + 1) % 3))
                    for s in range(NS):
                        until = min(NJ, NJ * (s + 1) // MAX_SLOTS) if ahead else 0

                        def next_job(job):
                            if job < until:
                                max_job(base(u) + task_of(job), ring + task_of(job), (r + 1) % 3, job)
                                return job + 1
                            return job

                        for half in range(2):
                            if s:
                                scores(U, r, s, half)
                            job = next_job(job)
                        if s:
                            values(U, r, s - 1)
                        while job < until:
                            job = next_job(job)
                        if s == 6:
                            at = OUT0_AT if ahead else 0
                            transpose_out(U, 0, base(u) + at, ring + at)
                    values(U, r, NS - 1)
                    if ahead:
                        first_scores(U + 1, (r + 1) % 3)
                    at = NJ + 1 if ahead else 1
                    transpose_out(U, 1, base(u) + at, ring + at)

                pe.wait_ge(s_stk[0], stack_count(L, 0, 0))
                for j in range(NJ):
                    max_job(L * LAYER_JOBS + j, j + 1, 0, j)
                first_scores(L * NU, 0)
                with pe.Fori(0, 5) as i:
                    for r in range(3):
                        step(i, r)
                step(5, 0, ahead=False)
                phase_end(pe, L, 2)

                pe.wait_ge(s_bo, (L + 1) * 32)
                apart(pe)
                with pe.Fori(0, NBLK // 2) as i:
                    for r in range(2):
                        n = L * NBLK + i * 2 + r
                        pe.wait_ge(s_mc, n + 1)
                        pe.wait_ge(s_mev, n + 1)
                        for f in range(KD):
                            for j in range(TPB):
                                last = tr(ps[:, 2 * r + f, j * P:j * P + P], mtok[:, r, j, f * P:f * P + P],
                                          ident[:, :])
                        last.then_inc(s_mtp, 1)
                    for r in range(2):
                        n = L * NBLK + i * 2 + r
                        pe.wait_ge(s_mev, n + 1 + 2)
                        pe.wait_ge(s_ma, n + 1)
                        for j in range(TPB):
                            for k in range(KD):
                                last = mm(ps[:, 4 + 2 * r + j // 2, (j % 2) * D:(j % 2) * D + D],
                                          mT[:, r, k, j * P:j * P + P], wo[:, k * D:k * D + D],
                                          start=k == 0 and j % 2 == 0, stop=k == KD - 1, skip_group_check=True)
                        last.then_inc(s_mo, 1)
                phase_end(pe, L, 3)
                norm(L * 2 + 1)
                phase_end(pe, L, 4)

                with pe.Fori(0, NBLK // 2) as i:
                    for r in range(2):
                        pe.wait_ge(s_lge, L * NBLK + i * 2 + r + 1)
                        for e, (ws, xs) in enumerate(PRODUCTS):
                            for k in range(KD):
                                last = mm(ps[:, r, :], hsp[:, 0, ws, k * P:k * P + P],
                                          xT[:, k, xs, ds((i * 2 + r) * BLK, BLK)],
                                          start=e == 0 and k == 0, stop=e == 2 and k == KD - 1)
                        last.then_inc(s_lg, 1)
                    for r in range(2):
                        n = L * NBLK + i * 2 + r
                        pe.wait_ge(s_lge, n + 1 + 2)
                        pe.wait_ge(s_lgd, n + 1)
                        apart(pe)
                        for j in range(TPB):
                            last = tr(ps[:, 2 + r, j * NE:j * NE + NE], lgT[0:NE, r, j * P:j * P + P],
                                      ident[0:NE, 0:NE])
                        last.then_inc(s_lgt, 1)
                pe.wait_ge(s_gs, L + 1)
                for n in range(NBLK):
                    pe.wait_ge(s_gd, L * NBLK + n + 1)
                    for j in range(TPB):
                        last = tr(ps[:, n % 2, 64 * j:64 * j + 64].bitcast(BF16), gst[:, n * TPB + j, :], identb[:, :])
                    last.then_inc(s_gt, 1)
                phase_end(pe, L, 5)

                def group(g, chunks, first_n, first_y, first_w):
                    def gate_rows(blk, c):
                        Q = first_n + blk * chunks + c
                        pe.wait_ge(s_hg, Q + 3 - slot_age(c, chunks, 2))
                        mm(ps[:, 3 + c % 2, :], sel[:, ds((g * NCH + c) * P, P)], gT[:, ds(blk * BLK, BLK)],
                           start=True, stop=True).then_inc(s_g, 1)

                    def hidden(blk, c):
                        Q = first_n + blk * chunks + c
                        pe.wait_ge(s_r, Q + 4 - slot_age(c, chunks, 3))
                        for e, (ws, xs) in enumerate(PRODUCTS):
                            for k in range(KD):
                                last = mm(ps[:, c % 3, :], w1s[:, c, k, ws, :], xT[:, k, xs, ds(blk * BLK, BLK)],
                                          start=e == 0 and k == 0, stop=e == 2 and k == KD - 1)
                        last.then_inc(s_h, 1)

                    def summed(blk, c):
                        Q = first_n + blk * chunks + c
                        pe.wait_ge(s_lo, Q + 1 + 3)
                        for f in range(KD):
                            if c == 0:
                                pe.wait_ge(s_ye, (first_y + blk) * KD + f + 1)
                                if chunks == NCS:
                                    for s in range(3):
                                        mm(ps[:, 5 + f, :], b2s[:, s, f * P:f * P + P], gT[:, ds(blk * BLK, BLK)],
                                           start=s == 0, stop=False)
                            for e, (ws, xs) in enumerate(PRODUCTS):
                                last = mm(ps[:, 5 + f, :], w2s[:, c, ws, f * P:f * P + P], hsp[:, c % 3, xs, :],
                                          start=c == 0 and e == 0 and chunks != NCS, stop=c == chunks - 1 and e == 2)
                            if c == chunks - 1 and f == 0:
                                last.then_inc(s_y0, 1)
                        last.then_inc(s_m2, 1)

                    def transpose_out(blk, f):
                        Y = first_y + blk
                        pe.wait_ge(s_ye, (Y + 1) * KD + KD)
                        pe.wait_ge(s_ya, Y * 2 + f + 1)
                        for j in range(2):
                            for k in range(KD):
                                last = tr(ps[:, 7, (j * KD + k) * P:(j * KD + k) * P + P],
                                          ysb[:, k, (2 * f + j) * P:(2 * f + j) * P + P], ident[:, :])
                        last.then_inc(s_yt, 1)

                    def blk_body(blk, lagged, load_w):
                        for c in range(chunks):
                            gate_rows(blk, c)
                            if load_w:
                                pe.wait_ge(s_wl, first_w + c + 1 + 11)
                            hidden(blk, c)
                            if c >= 2:
                                summed(blk, c - 2)
                            elif lagged:
                                summed(blk - 1, chunks - 2 + c)
                            if lagged and c == 2:
                                transpose_out(blk - 1, 0)
                            if lagged and c == min(chunks - 1, 4):
                                transpose_out(blk - 1, 1)
                    blk_body(0, False, True)
                    with pe.Fori(1, NBLK) as blk:
                        blk_body(blk, True, False)
                    summed(NBLK - 1, chunks - 2)
                    summed(NBLK - 1, chunks - 1)
                    transpose_out(NBLK - 1, 0)
                    transpose_out(NBLK - 1, 1)

                with pe.Fori(0, NG) as g:
                    group(g, NCH, L * CHUNKS * NBLK + g * NCH * NBLK, L * (NG + 1) * NBLK + g * NBLK,
                          L * CHUNKS + g * NCH)
                group(NG, NCS, L * CHUNKS * NBLK + NG * NCH * NBLK, L * (NG + 1) * NBLK + NG * NBLK,
                      L * CHUNKS + NG * NCH)
                phase_end(pe, L, 6)


_SHAPES = dict(
    x=(B, T, D), wqkv=(NL, 3, D, D), bqkv=(NL, P, 6), wo=(NL, D, D), bo=(NL, D),
    rw=(D, P), rb=(P, 1), w1=(D, HIDS), w2=(HIDS, D), b1=(P, CHUNKS), b2=(NE + 32, D),
    rows=(NL, 2, SROWS - 48, T), ident=(P, P), masks=(2, P, P), sel=(P, HIDS))


def arrays(i):
    f = np.float32
    i = {k: np.asarray(v) for k, v in i.items()}
    A, Bp, F = "L0_attn_a_", "L0_attn_b_", "L0_ffn_"
    r = {"x": i[A + "x"]}
    r["wqkv"] = np.stack([np.stack([i[A + "k_w"].T, i[A + "q_w"].T, i[A + "v_w"].T]),
                          np.stack([i[Bp + "Wq"], i[Bp + "Wk"], i[Bp + "Wv"]])])
    bias = np.stack([np.stack([i[A + "k_b"], i[A + "q_b"], i[A + "v_b"]]),
                     np.stack([i[Bp + "bq"], i[Bp + "bk"], i[Bp + "bv"]])])
    r["bqkv"] = bias.reshape(NL, 6, P).transpose(0, 2, 1)
    r["wo"] = np.stack([i[A + "o_w"].T, i[Bp + "Wo"]])
    r["bo"] = np.stack([i[A + "o_b"], i[Bp + "bo"]])
    rw = np.zeros((D, P), f)
    rw[:, :NE] = i[F + "router_w"]
    r["rw"] = rw
    rb = np.zeros((P, 1), f)
    rb[:NE, 0] = i[F + "router_b"]
    r["rb"] = rb
    w1 = np.zeros((D, HIDS), f)
    w2 = np.zeros((HIDS, D), f)
    b1 = np.zeros((HIDS,), f)
    n, m = NE * HID, (NE + NSH) * HID
    w1[:, :n] = i[F + "rw1"].transpose(1, 0, 2).reshape(D, n)
    w1[:, n:m] = i[F + "sw1"].transpose(1, 0, 2).reshape(D, m - n)
    w2[:n] = i[F + "rw2"].reshape(n, D)
    w2[n:m] = i[F + "sw2"].reshape(m - n, D)
    b1[:n] = i[F + "rb1"].reshape(n)
    b1[n:m] = i[F + "sb1"].reshape(m - n)
    r["w1"], r["w2"], r["b1"] = w1, w2, b1.reshape(CHUNKS, P).T
    b2 = np.zeros((NE + 32, D), f)
    b2[:NE] = i[F + "rb2"]
    b2[NE:NE + NSH] = i[F + "sb2"]
    r["b2"] = b2
    t = np.arange(T, dtype=f)
    rows = np.zeros((NL, 2, SROWS - 48, T), f)
    rows[0, 0, 16], rows[0, 0, 17] = -t, 1.0
    rows[0, 1, 16], rows[0, 1, 17] = 1.0, t
    rows[:, 1, 18:20] = 1.0
    r["rows"] = rows
    r["ident"] = np.eye(P, dtype=f)
    q, k = np.arange(P)[:, None], np.arange(P)[None, :]
    r["masks"] = np.stack([np.where(k > q, NEG, 0.0), np.where(q > k, NEG, 0.0)]).astype(f)
    sel = np.zeros((P, HIDS), np.float16)
    for e in range(NE + NSH):
        for row in ((e, NE + e, 2 * NE + e) if e < NE else (3 * NE + e - NE,)):
            sel[row, e * HID:(e + 1) * HID] = 1.0
    r["sel"] = sel
    return {k: np.ascontiguousarray(v) for k, v in r.items()}


def kernel(**inputs):
    import concourse.bacc as _bacc
    from concourse.bass_utils import run_bass_kernel_spmd as _run

    nc = _bacc.Bacc("TRN2", target_bir_lowering=False, num_devices=1)
    laid = arrays(inputs)
    aps = {k: nc.dram_tensor(f"in_{k}", shape, F16 if k == "sel" else F32, kind="ExternalInput").ap()
           for k, shape in _SHAPES.items()}
    out = nc.dram_tensor("out_0", (B, T, D), F32, kind="ExternalOutput").ap()
    build(nc, aps, out)
    r = _run(nc, [{f"in_{k}": laid[k] for k in _SHAPES}], core_ids=[0])
    return r.results[0]["out_0"]
```

```python
from contextlib import ExitStack

import numpy as np

import concourse.bass as bass
from concourse import mybir

F32 = mybir.dt.float32
F32R = mybir.dt.float32r
BF16 = mybir.dt.bfloat16
F16 = mybir.dt.float16
ALU = mybir.AluOpType
ACT = mybir.ActivationFunctionType
AX = mybir.AxisListType
ds = bass.ds

P = 128
B, T, D = 4, 1024, 256
H, HD = 16, 16
NL = 2
NTOK = B * T
NT = NTOK // P
BLK = 512
NBLK = NTOK // BLK
TPB = BLK // P
KD = D // P
EPS = 1e-5
NEG = -(2.0 ** 100)

NE, NSH, TOPK, HID = 32, 2, 6, 176
NCH = 11
NG = NE * HID // (NCH * P)
NCS = 3
CHUNKS = NG * NCH + NCS
HIDS = CHUNKS * P

HG = 4
NU = B * H // HG
NQB = T // P
SROWS = 68

NPHASE = 5
ENGINES = 5


def max_jobs():
    jobs = []
    for i in range(NQB):
        first = 0
        if i >= 4:
            jobs += [(i, 0, BLK, [h]) for h in range(HG)]
            first = BLK
        w = (i + 1) * P - first
        per = min(HG, BLK // w)
        jobs += [(i, first, w, list(range(h, min(h + per, HG)))) for h in range(0, HG, per)]
    return jobs


def slot_age(c, chunks, ring):
    if c >= ring:
        return ring
    return c + chunks - max(k for k in range(chunks) if k % ring == c % ring)


def raw_count(L, g, c):
    if isinstance(g, int) and g == NG:
        return 32 * (L * 9 + 9)
    if c < 3:
        return 32 * (L * 9 + g * 2 + 1)
    if c >= 8:
        return 32 * (L * 9 + g * 2 + 2)
    return 32 * (L * 4 + g + 1)


def stack_count(L, turn, r):
    return (L * (6, 5, 5)[r] + turn + 1) * 112


def task_of(j):
    return j if j < OUT0_AT else j + 1


def exp_slots():
    return [(qt, kb, BLK if kb < 4 * qt else BLK - (kb - 4 * qt) * P)
            for qt in range(T // BLK) for kb in range(4 * qt + 4)]


MAX_JOBS = max_jobs()
SLOTS = exp_slots()
NJ, NS = len(MAX_JOBS), len(SLOTS)
WHEAD = 8
FIRST_WHEAD = 3
MAX_SLOTS = 8
STEP_JOBS = NJ + 3
OUT0_AT = NJ * 7 // MAX_SLOTS
MAX_AT, OUT1_AT = NJ + 1, NJ + 2
LAYER_JOBS = NJ + 1 + (NU - 1) * STEP_JOBS + 2
JOB_BANKS = (4, 5, 7)
STEP_LINKS = 3
CHAIN = 85
XB = KD * 2 * BLK
PRODUCTS = ((0, 0), (0, 1), (1, 0))
Q_SCALE = HD ** -0.5


def build(nc, a, out):
    qks = nc.dram_tensor("qks_scratch", (2, 2, NU, 64, T), F32, kind="Internal").ap()
    vds = nc.dram_tensor("v_scratch", (NU, P, NQB, HG * 32), F32, kind="Internal").ap()

    rows_scratch = nc.dram_tensor("rows_scratch", (NL, 2, SROWS - 48, T), F32, kind="Internal").ap()

    ctx = ExitStack()
    with ctx:
        def sb(name, shape, dt):
            return ctx.enter_context(nc.sbuf_tensor(name, shape, dt))

        def sem(name):
            return ctx.enter_context(nc.semaphore(name))

        split = sb("split", [P, 30720], F32R)
        xT = split[:, 0:XB * NBLK]
        wreg = split[:, 16384:27648]
        hsp = split[:, 27648:30720].rearrange("p (r s t) -> p r s t", r=3, s=2)
        stack = split[:, 0:24576].rearrange("p (r o h t) -> p r o h t", r=3, o=2, h=HG)
        stack32 = stack.bitcast(F32)
        vreg = split[:, 24576:27648].bitcast(F32).rearrange("p (r t h c) -> p r t h c", r=3, t=NQB, h=HG)
        wqkv = wreg[:, 0:3072].rearrange("p (m k s n) -> p m k s n", m=3, k=KD, s=2)
        qkst = wreg[:, 3072:11264].rearrange("p (r m s f t) -> p r m s f t", r=2, m=2, s=2, f=2)
        w1s = wreg.rearrange("p (c j) -> p c j", j=1024)[:, :, 0:512].rearrange(
            "p c (k s n) -> p c k s n", k=KD, s=2)
        w2s = wreg.rearrange("p (c j) -> p c j", j=1024)[:, :, 512:1024].rearrange(
            "p c (s n) -> p c s n", s=2)

        x = sb("x", [P, NT * D], F32)
        work = sb("work", [P, 12288], F32)
        attn = work[:, 0:8192].rearrange("p (f t c) -> p f t c", f=NU // 2, t=NQB)
        pexp = work[:, 8192:12288].rearrange("p (r h t) -> p r h t", r=4, h=2)
        xn = work[:, 8192:10240].rearrange("p (r t d) -> p r t d", r=2, t=TPB)
        fqk = work[:, 0:2048].rearrange("p (r f t) -> p r f t", r=2, f=2)
        vst = work[:, 2048:6144].rearrange("p (r t h c) -> p r t h c", r=2, t=TPB, h=H)
        vf = work[:, 6144:8192].rearrange("p (r f t) -> p r f t", r=2, f=2)
        mask32 = work[:, 0:2 * P].rearrange("p (m k) -> p m k", m=2)
        wraw = work[:, 10240:11776].rearrange("p (m k n) -> p m k n", m=3, k=KD)
        mT = work[:, 10240:12288].rearrange("p (r k t) -> p r k t", r=2, k=KD)
        gT = work[:, 0:2048].bitcast(BF16)
        sel = work[:, 2048:2048 + HIDS // 2].bitcast(F16)
        hbuf = work[:, 5120:6656].rearrange("p (r t) -> p r t", r=3)
        ysb = work[:, 6656:7680].rearrange("p (f t) -> p f t", f=KD)
        raw = work[:, 7680:11776].rearrange("p (r n) -> p r n", r=8)
        b2s = work[:, 11776:12160].bitcast(BF16).rearrange("p (s d) -> p s d", s=3)
        lgt = work[:, 5120:6208].rearrange("p (t e) -> p t e", e=NE + 2)
        prb = work[:, 6208:7296].rearrange("p (t e) -> p t e", e=NE + 2)
        rep = work[:, 7296:8384].rearrange("p (t e) -> p t e", e=NE + 2)
        gst = work[:, 8384:10432].bitcast(BF16).rearrange("p (t c) -> p t c", c=P)
        lgT = work[:, 10432:11456].rearrange("p (r t) -> p r t", r=2)
        top = work[:, 11456:11712].rearrange("p (t e) -> p t e", e=8)
        b2f = work[:, 5120:5888].rearrange("p (s d) -> p s d", s=3)

        osb = sb("osb", [P, BLK], F32)
        wo = osb
        sv = work[:, 11968:12288].rearrange("p (s t) -> p s t", s=10)
        small = sb("small", [P, 600], F32)
        stat = small[:, 0:192].rearrange("p (t s) -> p t s", s=6)
        mpart = small[:, 0:64].rearrange("p (s c) -> p s c", s=2)
        mneg = small[:, 64:96]
        mhl = split[0:32, 27648:27904].rearrange("p (s t) -> p s t", s=2)
        rden = small[:, 176:208].rearrange("p (r c) -> p r c", r=2)
        bqkv = small[:, 208:214]
        bq4 = small[:, 214:216]
        b1 = small[:, 216:216 + CHUNKS]
        rb = small[:, 264:265]
        bo = small[:, 272:528]
        mx8 = small[:, 528:560]
        sm8 = small[:, 560:592]
        ident = sb("ident", [P, P], F32)
        identb = sb("identb", [P, P], BF16)
        maskq = sb("maskq", [P, P], BF16)
        maskk = sb("maskk", [P, P], BF16)

        ps = ctx.enter_context(nc.psum_tensor("ps", [P, 8, BLK], F32))

        s_const, s_phase = sem("const_loaded"), sem("phase_done")
        s_x = [sem(f"x_loaded{q}") for q in range(4)]
        s_apart = sem("wait_carrier")
        s_chain = sem("dve_chain")
        s_stats = sem("input_statistics")
        s_var, s_sd = sem("var_ready"), sem("sd_ready")
        s_xn, s_tp, s_xh, s_xl = sem("xn_ready"), sem("xT_psum_ready"), sem("xT_hi_done"), sem("xT_lo_done")
        s_wload, s_wsplit = sem("qkv_weights_loaded"), sem("qkv_weights_split")
        s_pj, s_pf = sem("proj_ready"), sem("proj_evacuated")
        s_ph, s_pl, s_pd = sem("qk_hi_done"), sem("qk_lo_done"), [sem(f"qk_stored{r}") for r in range(2)]
        s_vt, s_vs, s_vd = sem("v_transposed"), sem("v_staged"), [sem(f"v_stored{r}") for r in range(2)]
        s_rows = [sem(f"constant_rows_loaded{r}") for r in range(3)]
        s_zero = [sem(f"stack_zeroed{r}") for r in range(3)]
        s_zq = sem("first_query_stack_zeroed")
        s_vl = [sem(f"values_loaded{r}") for r in range(3)]
        s_stk = [sem(f"stack_loaded{r}") for r in range(3)]
        s_st, s_pe, s_pv = sem("scoresT_ready"), sem("exp_done"), sem("values_done")
        s_mj, s_mr = sem("task_ready"), sem("task_done")
        s_neg, s_mrow = sem("neg_max_gathered"), sem("neg_max_rows_loaded")
        s_ov = sem("out_evacuated")
        s_bo, s_bod = sem("merge_bias_loaded"), sem("merge_bias_added")
        s_mtp, s_mev, s_mo, s_ma = (sem("merge_transposed"), sem("merge_evacuated"), sem("merge_product"),
                                    sem("merge_added"))
        s_rld, s_rsp = sem("router_loaded"), sem("router_split")
        s_lg, s_lge, s_lgt, s_lgd = (sem("logitsT_ready"), sem("logitsT_evacuated"),
                                     sem("logits_transposed"), sem("logits_stored"))
        s_le, s_ee, s_gs, s_gt, s_gd = (sem("logits_shifted"), sem("logits_exp"), sem("gates_split"),
                                        sem("gates_transposed"), sem("gatesT_stored"))
        s_raw = [sem(f"expert_raw_loaded{r}") for r in range(8)]
        s_wh, s_wl = sem("expert_hi_done"), sem("expert_lo_done")
        s_m2, s_y0 = sem("chunk_summed"), sem("first_half_summed")
        s_g, s_h, s_r, s_hg, s_hi, s_lo = (sem("gate_rows_ready"), sem("hidden_ready"), sem("relu_done"),
                                           sem("gated_done"), sem("hidden_hi_done"), sem("hidden_lo_done"))
        s_ye, s_yt, s_ya = sem("out_copied"), sem("outT_ready"), sem("out_added")
        s_out = sem("result_stored")
        block = ctx.enter_context(nc.Block())

        def x_part(blk, k, s):
            return xT[:, ds(blk * XB + (k * 2 + s) * BLK, BLK)]

        def x_parts(blk, s):
            return xT[:, ds(blk * XB, XB)].rearrange("p (k s t) -> p k s t", k=KD, s=2)[:, :, s, :]

        def apart(e):
            e.sem_inc(s_apart, 1)

        def phase_end(e, L, n):
            apart(e)
            e.drain().then_inc(s_phase, 1)
            e.wait_ge(s_phase, (L * NPHASE + n + 1) * ENGINES)
            apart(e)

        @block.sync
        def _(sp):
            xv = x[:, :].rearrange("p (t d) -> p t d", d=D)
            xin = a["x"].rearrange("b (t p) d -> p (b t) d", p=P)
            for q in range(4):
                sp.dma_start(xv[:, 8 * q:8 * q + 8, :], xin[:, 8 * q:8 * q + 8, :]).then_inc(s_x[q], 16)
            sp.dma_start(ident[:, :], a["ident"]).then_inc(s_const, 16)
            sp.dma_start(mask32, a["masks"].rearrange("m p k -> p m k")).then_inc(s_const, 16)
            sp.dma_start(rows_scratch, a["rows"]).then_inc(s_const, 16)

            with sp.Fori(0, NL) as L:
                for m in range(3):
                    sp.dma_start(wraw[:, m], a["wqkv"][L, m].rearrange("(k p) n -> p k n", p=P)).then_inc(s_wload, 16)
                sp.dma_start(bqkv, a["bqkv"][L]).then_inc(s_wload, 16)
                sp.dma_start(bo, a["bo"][ds(L, 1)].partition_broadcast(P).rearrange("p o d -> p (o d)")).then_inc(s_bo, 16)
                def store_batch(b):
                    for r in range(2):
                        n = L * NBLK + b * 2 + r
                        sp.wait_ge(s_pl, n * 4 + 4 + 4)
                        apart(sp)
                        for m in range(2):
                            for s in range(2):
                                sp.dma_start(
                                    qks[m, s, ds(b * HG, HG), :, r * BLK:(r + 1) * BLK]
                                    .rearrange("(f e) w t -> (e w) f t", f=2),
                                    qkst[:, r, m, s].bitcast(F32)).then_inc(s_pd[r], 16)
                        sp.wait_ge(s_vs, n + 1 + 1)
                        for u in range(HG):
                            sp.dma_start(
                                vds[b * HG + u, :, r * TPB:(r + 1) * TPB, :],
                                vst[:, r, :, HG * u:HG * u + HG, :].rearrange("p t h c -> p t (h c)")
                            ).then_inc(s_vd[r], 16)
                def load_rows(r):
                    sp.wait_ge(s_zero[r], (L + 1) * (1 if r == 0 else 2))
                    if r == 0:
                        sp.wait_ge(s_zq, L + 1)
                    for o in range(2):
                        sp.dma_start(stack32[48:SROWS, r, o], rows_scratch[L, o].unsqueeze(1)
                                     .broadcast_to([SROWS - 48, HG, T])).then_inc(s_rows[r], 16)

                def load_stack(u, r):
                    for o in range(2):
                        for g, s in enumerate(((0, 0, 1), (0, 1, 0))[o]):
                            sp.dma_start(stack32[16 * g:16 * g + 16, r, o],
                                         qks[o, s, u].rearrange("(h w) t -> w h t", h=HG)).then_inc(s_stk[r], 16)
                    sp.wait_ge(s_rows[r], (L + 1) * 32)
                    sp.dma_start(stack32[66:68, r, 0], rows_scratch[L, 0, 0:2].unsqueeze(1)
                                 .broadcast_to([2, HG, T])).then_inc(s_stk[r], 16)

                def load_values(u, r):
                    sp.dma_start(vreg[:, r], vds[u].rearrange("p t (h c) -> p t h c", h=HG)).then_inc(s_vl[r], 16)

                def load_unit(u, r):
                    sp.wait_ge(s_pv, (L * NU + u - 2) * NS + 2)
                    load_stack(u, r)
                    load_values(u, r)

                with sp.Fori(0, B - 1) as b:
                    store_batch(b)
                sp.wait_ge(s_const, 48)
                load_rows(0)
                for r in range(2):
                    sp.wait_ge(s_pd[r], (L * B + 1) * 64 + 64)
                load_stack(0, 0)
                store_batch(B - 1)
                phase_end(sp, L, 0)

                for r in range(2):
                    sp.wait_ge(s_pd[r], (L * B + B) * 64 + 64)
                    sp.wait_ge(s_vd[r], (L * B + B) * 64 + 64)
                def load_neg_max(u, r, task):
                    sp.wait_ge(s_mr, L * LAYER_JOBS + task + 1 + 3)
                    for s in range(2):
                        sp.dma_start(stack32[66 + s:67 + s, r, 0].rearrange("p h t -> p (h t)"),
                                     mhl[:, s, :].bitcast(F32)).then_inc(s_mrow, 16)

                def max_task(u):
                    return NJ + 1 + (u - 1) * STEP_JOBS + MAX_AT

                load_values(0, 0)
                for r in (1, 2):
                    load_rows(r)
                    load_stack(r, r)
                    load_values(r, r)
                    if r == 1:
                        load_neg_max(0, 0, NJ)
                with sp.Fori(0, 4) as i:
                    for r in range(3):
                        load_neg_max(i * 3 + r + 1, (r + 1) % 3, max_task(i * 3 + r + 1))
                        load_unit(i * 3 + r + 3, r)
                load_neg_max(13, 1, max_task(13))
                load_unit(15, 0)
                load_neg_max(14, 2, max_task(14))
                load_neg_max(15, 0, max_task(15))
                phase_end(sp, L, 1)
                sp.dma_start(wo[:, :].rearrange("p (k n) -> p k n", k=KD),
                             a["wo"][L].rearrange("(k p) n -> p k n", p=P)).then_inc(s_bo, 16)
                phase_end(sp, L, 2)

                sp.dma_start(raw[:, 0, 0:256].rearrange("p (k n) -> p k n", k=KD),
                             a["rw"].rearrange("(k p) n -> p k n", p=P)).then_inc(s_rld, 16)
                sp.dma_start(rb, a["rb"]).then_inc(s_rld, 16)
                sp.dma_start(b1, a["b1"]).then_inc(s_rld, 16)
                sp.dma_start(sel, a["sel"]).then_inc(s_rld, 16)
                sp.wait_ge(s_gs, (L + 1) * 1)
                for s in range(3):
                    sp.dma_start(b2f[32 * s:32 * s + 32, 0, :], a["b2"][0:NE]).then_inc(s_rld, 16)
                sp.dma_start(b2f[96:128, 0, :], a["b2"][NE:NE + 32]).then_inc(s_rld, 16)
                phase_end(sp, L, 3)

                def load_chunk(col, c, n):
                    r = c % 8
                    sp.wait_ge(s_wl, n)
                    sp.dma_start(raw[:, r, 0:256].rearrange("p (k n) -> p k n", k=KD),
                                 a["w1"][:, ds(col, P)].rearrange("(k p) n -> p k n", p=P)).then_inc(s_raw[r], 16)
                    sp.dma_start(raw[:, r, 256:512], a["w2"][ds(col, P), :]).then_inc(s_raw[r], 16)

                with sp.Fori(0, NG) as g:
                    for c in range(NCH):
                        n = L * CHUNKS + g * NCH + c
                        n = n - 8 if c >= 8 else (n + 8 - NCH if c + 8 < NCH else n - NCH)
                        load_chunk((g * NCH + c) * P, c, n + 1 + 11)
                for c in range(NCS):
                    load_chunk((NG * NCH + c) * P, c, L * CHUNKS + NG * NCH + c + 8 - NCH + 1 + 11)
                phase_end(sp, L, 4)

            xo = out.rearrange("b (t p) d -> p (b t) d", p=P)
            for q in range(4):
                sp.dma_start(xo[:, 8 * q:8 * q + 8, :], xv[:, 8 * q:8 * q + 8, :]).then_inc(s_out, 16)
            sp.wait_ge(s_out, 64)

        @block.vector
        def _(dve):
            v = nc.vector
            dve.sem_inc(s_xl, 2)
            dve.sem_inc(s_vs, 1)
            dve.sem_inc(s_mr, 3)
            dve.sem_inc(s_ma, 2)
            dve.sem_inc(s_lgd, 2)
            dve.sem_inc(s_gd, 2)
            dve.sem_inc(s_hg, 2)
            dve.sem_inc(s_ya, 1)
            chain = [0]
            turns = [0]

            def link(ins):
                chain[0] += 1
                ins.then_inc(s_chain, 1)

            def statistics(tile, tiles):
                for j in range(tiles):
                    last = v.bn_stats(stat[:, ds(tile + j, 1), :].rearrange("p t s -> p (t s)"),
                                      x[:, ds((tile + j) * D, D)])
                return last

            for q in range(4):
                dve.wait_ge(s_x[q], 16)
                last = statistics(q * NT // 4, NT // 4)
            last.then_inc(s_stats, 1)
            dve.wait_ge(s_const, 48)
            v.tensor_copy(identb[:, :], ident[:, :])
            v.tensor_copy(maskq[:, :], mask32[:, 0, :])
            v.tensor_copy(maskk[:, :], mask32[:, 1, :])
            dve.wait_ge(s_stats, 1)

            with dve.Fori(0, NL) as L:
                chain[0] = 0

                def linked():
                    dve.wait_ge(s_chain, L * CHAIN + turns[0] + chain[0])

                def row_scales(k):
                    me, ve, mo, vo = (stat[:, :, s] for s in (1, 2, 4, 5))
                    v.tensor_tensor(sv[:, 0], me, mo, ALU.subtract)
                    v.tensor_tensor(sv[:, 1], me, mo, ALU.add)
                    link(v.tensor_tensor(sv[:, 2], ve, vo, ALU.add))
                    linked()
                    v.tensor_tensor(sv[:, 3], sv[:, 0], sv[:, 0], ALU.mult)
                    link(v.tensor_scalar(sv[:, 4], sv[:, 2], 1.0 / D, EPS, ALU.mult, ALU.add))
                    linked()
                    v.scalar_tensor_tensor(sv[:, 5], sv[:, 3], 0.25, sv[:, 4], ALU.mult, ALU.add).then_inc(s_var, 1)
                    dve.wait_ge(s_sd, k + 1)
                    link(v.reciprocal(sv[:, 7], sv[:, 6]))
                    linked()
                    link(v.tensor_tensor(sv[:, 7], sv[:, 5], sv[:, 7], ALU.mult))
                    linked()
                    link(v.tensor_tensor(sv[:, 7], sv[:, 6], sv[:, 7], ALU.add))
                    linked()
                    link(v.reciprocal(sv[:, 7], sv[:, 7]))
                    linked()
                    link(v.tensor_scalar(sv[:, 8], sv[:, 7], 2.0, None, ALU.mult))
                    linked()
                    link(v.scalar_tensor_tensor(sv[:, 9], sv[:, 1], -0.5, sv[:, 8], ALU.mult, ALU.mult))
                    linked()
                    apart(dve)

                def normalise_block(k, blk, r):
                    dve.wait_ge(s_tp, k * NBLK + blk + 1)
                    for j in range(TPB):
                        t = blk * TPB + j
                        last = v.tensor_scalar(xn[:, r, j, :], x[:, ds(t * D, D)], sv[:, 8, ds(t, 1)],
                                               sv[:, 9, ds(t, 1)], ALU.mult, ALU.add)
                    last.then_inc(s_xn, 1)

                def x_lo(k, blk, r):
                    dve.wait_ge(s_xh, k * NBLK + blk + 1)
                    v.tensor_tensor(x_parts(blk, 1), ps[:, 2 + 2 * r:4 + 2 * r, :], x_parts(blk, 0).bitcast(F32),
                                    ALU.subtract).then_inc(s_xl, 1)

                row_scales(L * 2)
                normalise_block(L * 2, 0, 0)
                dve.wait_ge(s_wload, (L + 1) * 64)
                v.tensor_scalar(bq4, bqkv[:, 0:2], HD ** -0.5, None, ALU.mult)
                link(v.tensor_copy(wqkv[:, :, :, 0, :], wraw))
                linked()
                v.tensor_tensor(wqkv[:, :, :, 1, :], wraw, wqkv[:, :, :, 0, :].bitcast(F32),
                                ALU.subtract).then_inc(s_wsplit, 1)
                normalise_block(L * 2, 1, 1)
                v.memset(vst[:, :, :, :, HD:32], 1.0)
                x_lo(L * 2, 0, 0)
                normalise_block(L * 2, 2, 0)
                x_lo(L * 2, 1, 1)

                def qkv_block(b, r, ahead):
                    blk = b * 2 + r
                    n = L * NBLK + blk
                    dve.wait_ge(s_pd[r], (L * B + b) * 64 + 64)
                    for m in range(2):
                        for f in range(2):
                            dve.wait_ge(s_pf, n * 6 + m * 2 + f + 1 + 2)
                            v.tensor_copy(qkst[:, r, m, 0, f], fqk[:, m, f]).then_inc(s_ph, 1)
                    if ahead > 2:
                        normalise_block(L * 2, blk + 3, 1 - r)
                    if ahead > 1:
                        x_lo(L * 2, blk + 2, r)
                    dve.wait_ge(s_vd[r], (L * B + b) * 64 + 64)
                    dve.wait_ge(s_vt, n + 1 + 2)
                    for f in range(2):
                        last = v.tensor_copy(vst[:, r, :, 8 * f:8 * f + 8, 0:HD],
                                             ps[:, 6 + f, :].rearrange("p (t h c) -> p t h c", t=TPB, h=8))
                    last.then_inc(s_vs, 1)

                with dve.Fori(0, B - 2) as b:
                    for r in range(2):
                        qkv_block(b, r, 3)
                for r in range(2):
                    qkv_block(B - 2, r, 3 - r)
                dve.wait_ge(s_pj, (L * NBLK + 4) * 6)
                v.memset(stack32[64:P, 0, 0], 0.0).then_inc(s_zq, 1)
                for r in range(2):
                    qkv_block(B - 1, r, 1 - r)
                phase_end(dve, L, 0)

                def base(u):
                    return L * LAYER_JOBS + NJ + 1 + u * STEP_JOBS

                def max_job(task, ring, j):
                    i, first, w, heads = MAX_JOBS[j]
                    dve.wait_ge(s_mj, task + 1)
                    cols = mpart[:, 0 if first or i < 4 else 1, :].rearrange("p (h q) -> p h q", h=HG)
                    v.tensor_reduce(cols[:, heads[0]:heads[0] + len(heads), i],
                                    ps[:, JOB_BANKS[ring % 3], 0:w * len(heads)].rearrange("p (h k) -> p h k", k=w),
                                    AX.X, ALU.max, negate=True).then_inc(s_mr, 1)

                def split_max(u, task, ring):
                    late = mpart[:, :, :].rearrange("p s (h q) -> p s h q", h=HG)
                    neg = mneg.rearrange("p (h q) -> p h q", h=HG)
                    dve.wait_ge(s_mr, task + 3)
                    v.tensor_copy(neg[:, :, 0:4], late[:, 0, :, 0:4])
                    v.tensor_tensor(neg[:, :, 4:8], late[:, 0, :, 4:8], late[:, 1, :, 4:8],
                                    ALU.min).then_inc(s_neg, 1)
                    dve.wait_ge(s_mj, task + 1)
                    rows = ps[0:32, JOB_BANKS[ring % 3], 0:P]
                    link(v.tensor_copy(mhl[:, 0, :], rows))
                    linked()
                    v.tensor_tensor(mhl[:, 1, :], rows, mhl[:, 0, :].bitcast(F32), ALU.subtract).then_inc(s_mr, 1)

                def normalise(u, qt, task, ring):
                    dve.wait_ge(s_mj, task + 1)
                    o = ps[:, JOB_BANKS[ring % 3], :].rearrange("p (q h c) -> p q h c", q=4, h=HG)
                    rd = rden[:, qt].rearrange("p (q h) -> p q h", q=4)
                    link(v.reciprocal(rd, o[:, :, :, HD]))
                    linked()
                    tile = work[:, ds((u >> 1) * (NQB * P) + (u & 1) * (P // 2) + qt * (4 * P), 4 * P)]
                    v.tensor_tensor(
                        tile.rearrange("p (q c) -> p q c", q=4)[:, :, 0:P // 2].rearrange("p q (h c) -> p q h c", h=HG),
                        o[:, :, :, 0:HD], rd.unsqueeze(3).broadcast_to([P, 4, HG, HD]), ALU.mult).then_inc(s_mr, 1)

                def step(u, r):
                    ring = r * STEP_JOBS
                    for j in range(NJ):
                        if j == OUT0_AT:
                            normalise(u, 0, base(u) + j, ring + j)
                        max_job(base(u) + task_of(j), ring + task_of(j), j)
                    split_max(u + 1, base(u) + MAX_AT, ring + MAX_AT)
                    normalise(u, 1, base(u) + OUT1_AT, ring + OUT1_AT)

                for j in range(NJ):
                    max_job(L * LAYER_JOBS + j, j, j)
                split_max(0, L * LAYER_JOBS + NJ, NJ)
                with dve.Fori(0, 5) as i:
                    before = chain[0]
                    turns[0] = i * (3 * STEP_LINKS)
                    for r in range(3):
                        step(i * 3 + r, r)
                    turns[0] = 0
                    assert chain[0] == before + 3 * STEP_LINKS
                chain[0] += 4 * 3 * STEP_LINKS
                for qt in range(2):
                    normalise(NU - 1, qt, base(NU - 1) + qt, qt)
                phase_end(dve, L, 1)

                def merge_block(i, r):
                    n = L * NBLK + i * 2 + r
                    dve.wait_ge(s_mo, n + 1 + 2)
                    if r == 0:
                        dve.wait_ge(s_bod, (L + 1) * NT)
                    xb = x[:, ds((i * 2 + r) * TPB * D, TPB * D)]
                    v.tensor_tensor(xb, ps[:, 4 + 2 * r:6 + 2 * r, :].rearrange("p f t -> p (f t)"), xb,
                                    ALU.add).then_inc(s_ma, 1)
                    dve.wait_ge(s_ma, n + 1 + 2)
                    statistics((i * 2 + r) * TPB, TPB)

                with dve.Fori(0, NBLK // 2) as i:
                    for r in range(2):
                        merge_block(i, r)
                phase_end(dve, L, 2)
                row_scales(L * 2 + 1)
                normalise_block(L * 2 + 1, 0, 0)
                dve.wait_ge(s_rld, L * 128 + 64)
                link(v.tensor_copy(hsp[:, 0, 0, 0:256], raw[:, 0, 0:256]))
                linked()
                v.tensor_tensor(hsp[:, 0, 1, 0:256], raw[:, 0, 0:256], hsp[:, 0, 0, 0:256].bitcast(F32),
                                ALU.subtract).then_inc(s_rsp, 1)
                normalise_block(L * 2 + 1, 1, 1)
                x_lo(L * 2 + 1, 0, 0)
                normalise_block(L * 2 + 1, 2, 0)
                x_lo(L * 2 + 1, 1, 1)

                def route_block(i, r, ahead):
                    blk = i * 2 + r
                    if ahead > 2:
                        normalise_block(L * 2 + 1, blk + 3, 1 - r)
                    if ahead > 1:
                        x_lo(L * 2 + 1, blk + 2, r)
                    dve.wait_ge(s_lgt, L * NBLK + blk + 1 + 2)
                    v.tensor_copy(lgt[:, ds(blk * TPB, TPB), 0:NE],
                                  ps[:, 6 + r, 0:TPB * NE].rearrange("p (t e) -> p t e", e=NE)).then_inc(s_lgd, 1)

                with dve.Fori(0, NBLK // 2 - 2) as i:
                    for r in range(2):
                        route_block(i, r, 3)
                for n in range(4):
                    route_block(NBLK // 2 - 2 + n // 2, n % 2, 3 - n)
                dve.wait_ge(s_lgd, (L + 1) * NBLK + 2)
                link(v.tensor_reduce(mx8, lgt[:, :, 0:NE], AX.X, ALU.max))
                linked()
                v.tensor_tensor(lgt[:, :, 0:NE], lgt[:, :, 0:NE], mx8.unsqueeze(2).broadcast_to([P, NT, NE]),
                                ALU.subtract).then_inc(s_le, 1)
                dve.wait_ge(s_ee, L + 1)
                v.memset(prb[:, :, NE:NE + 2], -1.0)
                link(v.tensor_reduce(sm8, rep[:, :, 0:NE], AX.X, ALU.add))
                linked()
                link(v.reciprocal(sm8, sm8))
                linked()
                link(v.tensor_tensor(prb[:, :, 0:NE], rep[:, :, 0:NE], sm8.unsqueeze(2).broadcast_to([P, NT, NE]),
                                     ALU.mult))
                linked()
                apart(dve)
                for t in range(NT):
                    last = v.max(top[:, t, :], prb[:, t, :])
                link(last)
                linked()
                link(v.memset(top[:, :, TOPK:8], -1.0))
                linked()
                apart(dve)
                for t in range(NT):
                    last = v.match_replace(rep[:, t, :], top[:, t, :], prb[:, t, :], 0.0)
                link(last)
                linked()
                g = lgt[:, :, 0:NE]
                link(v.tensor_tensor(g, prb[:, :, 0:NE], rep[:, :, 0:NE], ALU.subtract))
                linked()
                link(v.tensor_reduce(sm8, g, AX.X, ALU.add))
                linked()
                link(v.reciprocal(sm8, sm8))
                linked()
                link(v.tensor_tensor(g, g, sm8.unsqueeze(2).broadcast_to([P, NT, NE]), ALU.mult))
                linked()
                v.memset(gst[:, :, 3 * NE:P], 0.0)
                link(v.tensor_copy(gst[:, :, 0:NE], g))
                linked()
                v.memset(gst[:, :, 3 * NE:3 * NE + NSH], 1.0 / NSH)
                link(v.tensor_tensor(g, g, gst[:, :, 0:NE], ALU.subtract))
                linked()
                link(v.tensor_copy(gst[:, :, NE:2 * NE], g))
                linked()
                link(v.tensor_tensor(g, g, gst[:, :, NE:2 * NE], ALU.subtract))
                linked()
                v.tensor_copy(gst[:, :, 2 * NE:3 * NE], g).then_inc(s_gs, 1)
                for n in range(NBLK):
                    dve.wait_ge(s_gt, L * NBLK + n + 1)
                    v.tensor_copy(gT[:, n * BLK:(n + 1) * BLK],
                                  ps[:, n % 2, 0:BLK // 2].bitcast(BF16)).then_inc(s_gd, 1)
                dve.wait_ge(s_rld, L * 128 + 128)
                link(v.tensor_copy(b2s[:, 0, :], b2f[:, 0, :]))
                linked()
                link(v.tensor_tensor(b2f[:, 1, :], b2f[:, 0, :], b2s[:, 0, :], ALU.subtract))
                linked()
                link(v.tensor_copy(b2s[:, 1, :], b2f[:, 1, :]))
                linked()
                link(v.tensor_tensor(b2f[:, 2, :], b2f[:, 1, :], b2s[:, 1, :], ALU.subtract))
                linked()
                v.tensor_copy(b2s[:, 2, :], b2f[:, 2, :])
                phase_end(dve, L, 3)

                def gate_mul(n, c, odd):
                    dve.wait_ge(s_r, n + c + 1 + 3)
                    dve.wait_ge(s_g, n + c + 1)
                    v.tensor_tensor(hbuf[:, c % 3, :], ps[:, 3 + (odd + c) % 2, :], hbuf[:, c % 3, :],
                                    ALU.mult).then_inc(s_hg, 1)

                def hidden_hi(n, c, before):
                    dve.wait_ge(s_hg, n + c + 1 + 2)
                    dve.wait_ge(s_m2, n + c + 4 - slot_age(c, before, 3))
                    v.tensor_copy(hsp[:, c % 3, 0, :], hbuf[:, c % 3, :]).then_inc(s_hi, 1)

                def out_add(yn, blk, final, f):
                    dve.wait_ge(s_yt, yn * 2 + f + 1 + 1)
                    xb = x[:, ds(blk * TPB * D + f * 512, 512)]
                    v.tensor_tensor(xb, ps[:, 7, :], xb, ALU.add).then_inc(s_ya, 1)
                    if final:
                        dve.wait_ge(s_ya, yn * 2 + f + 1 + 1)
                        statistics(blk * TPB + f * 2, 2)

                def weights_hi(g, c):
                    dve.wait_ge(s_raw[c % 8], raw_count(L, g, c))
                    v.tensor_copy(w1s[:, c, :, 0, :], raw[:, c % 8, 0:256].rearrange("p (k n) -> p k n", k=KD))
                    v.tensor_copy(w2s[:, c, 0, :], raw[:, c % 8, 256:512]).then_inc(s_wh, 1)

                def group(g, chunks, before, following):
                    first_n, first_y = (L * CHUNKS + g * NCH) * NBLK, (L * (NG + 1) + g) * NBLK
                    head = WHEAD if before else FIRST_WHEAD

                    def blk_body(blk, odd, first=False, last=False):
                        n = first_n + blk * chunks
                        lag = (first_y + blk - 1, blk - 1, chunks == NCS)
                        if first:
                            lag = (first_y - 1, NBLK - 1, False) if before else None
                        for c in range(chunks):
                            if first and head + c < chunks:
                                if before:
                                    dve.wait_ge(s_m2, first_n + head + c - NCH + 4)
                                weights_hi(g, head + c)
                            if lag and c == 2 and chunks == NCS:
                                out_add(*lag, 0)
                            gate_mul(n, c, odd)
                            hidden_hi(n, c, (before or NCH) if first else chunks)
                            if last and 0 <= c - 3 < min(WHEAD, following):
                                dve.wait_ge(s_m2, n + c - 3 + 4)
                                weights_hi(g + 1, c - 3)
                            if lag and c == 2 and chunks != NCS:
                                out_add(*lag, 0)
                            if lag and c == min(chunks - 1, 4):
                                out_add(*lag, 1)
                    blk_body(0, 0, first=True)
                    with dve.Fori(0, NBLK // 2 - 1) as i:
                        for odd in (1, 0):
                            blk_body(i * 2 + 2 - odd, odd)
                    blk_body(NBLK - 1, 1, last=True)
                    if not following:
                        for f in range(2):
                            out_add(first_y + NBLK - 1, NBLK - 1, chunks == NCS, f)

                for c in range(FIRST_WHEAD):
                    weights_hi(0, c)
                group(0, NCH, 0, NCH)
                with dve.Fori(1, NG - 1) as g:
                    group(g, NCH, NCH, NCH)
                group(NG - 1, NCH, NCH, NCS)
                group(NG, NCS, NCH, 0)
                phase_end(dve, L, 4)
            assert chain[0] == CHAIN, chain[0]

        @block.scalar
        def _(act):
            c = nc.scalar
            act.sem_inc(s_pf, 2)
            act.sem_inc(s_pe, 2)
            act.sem_inc(s_ov, 1)
            act.sem_inc(s_mev, 2)
            act.sem_inc(s_lge, 2)
            act.sem_inc(s_r, 3)
            act.sem_inc(s_ye, KD)
            with act.Fori(0, NL) as L:
                def root(k):
                    act.wait_ge(s_var, k + 1)
                    c.activation(sv[:, 6], sv[:, 5], ACT.Sqrt).then_inc(s_sd, 1)

                def x_hi(k, blk, r):
                    act.wait_ge(s_tp, k * NBLK + blk + 1 + 2)
                    c.activation(x_parts(blk, 0), ps[:, 2 + 2 * r:4 + 2 * r, :], ACT.Copy).then_inc(s_xh, 1)

                def qkv_block(b, r, ahead):
                    n = L * NBLK + b * 2 + r
                    for m in range(3):
                        for f in range(2):
                            j = m * 2 + f
                            act.wait_ge(s_pj, n * 6 + j + 1)
                            if m < 2:
                                act.wait_ge(s_pl, n * 4 + j + 1)
                            elif f == 0:
                                act.wait_ge(s_vt, n + 1)
                            c.activation(fqk[:, m, f] if m < 2 else vf[:, r, f], ps[:, j % 2, :], ACT.Identity,
                                         bias=bq4[:, f:f + 1] if m == 0 else bqkv[:, j:j + 1],
                                         scale=Q_SCALE if m == 0 else 1.0).then_inc(s_pf, 1)
                    if ahead:
                        x_hi(L * 2, b * 2 + r + 2, r)

                root(L * 2)
                x_hi(L * 2, 0, 0)
                x_hi(L * 2, 1, 1)
                act.wait_ge(s_wsplit, L + 1)
                with act.Fori(0, B - 1) as b:
                    for r in range(2):
                        qkv_block(b, r, True)
                for r in range(2):
                    qkv_block(B - 1, r, False)
                phase_end(act, L, 0)

                def evacuate(U, qt, tasks):
                    act.wait_ge(s_pv, U * NS + (4, NS)[qt] + 2)
                    act.wait_ge(s_mj, tasks)
                    c.activation(osb[:, :], ps[:, 6, :], ACT.Copy).then_inc(s_ov, 1)

                def step(u, out0_at):
                    U = L * NU + u
                    base = L * LAYER_JOBS + NJ + 1 + u * STEP_JOBS
                    for s, (qt, kb, w) in enumerate(SLOTS):
                        act.wait_ge(s_pv, U * NS + s + 1)
                        for h in range(2):
                            act.wait_ge(s_st, (U * NS + s) * 2 + h + 1)
                            c.activation(pexp[:, (s % 2) * 2 + h, :, BLK - w:], ps[:, 2 * h:2 * h + 2, BLK - w:],
                                         ACT.Exp).then_inc(s_pe, 1)
                        if s == 4:
                            evacuate(U, 0, base)
                    evacuate(U, 1, base + out0_at + 1)

                with act.Fori(0, 5) as i:
                    for r in range(3):
                        step(i * 3 + r, OUT0_AT)
                step(NU - 1, 0)
                phase_end(act, L, 1)

                with act.Fori(0, NBLK // 2) as i:
                    for r in range(2):
                        n = L * NBLK + i * 2 + r
                        act.wait_ge(s_mtp, n + 1 + 2)
                        act.wait_ge(s_mo, n + 1)
                        c.activation(mT[:, r], ps[:, 2 * r:2 * r + 2, :], ACT.Copy).then_inc(s_mev, 1)
                phase_end(act, L, 2)

                def route_block(i, r, ahead):
                    n = L * NBLK + i * 2 + r
                    act.wait_ge(s_lg, n + 1)
                    act.wait_ge(s_lgt, n + 1)
                    c.activation(lgT[0:NE, r, :], ps[0:NE, r, :], ACT.Identity,
                                 bias=rb[0:NE, :]).then_inc(s_lge, 1)
                    if ahead:
                        x_hi(L * 2 + 1, i * 2 + r + 2, r)

                root(L * 2 + 1)
                x_hi(L * 2 + 1, 0, 0)
                x_hi(L * 2 + 1, 1, 1)
                act.wait_ge(s_rld, L * 128 + 64)
                with act.Fori(0, NBLK // 2 - 1) as i:
                    for r in range(2):
                        route_block(i, r, True)
                for r in range(2):
                    route_block(NBLK // 2 - 1, r, False)
                act.wait_ge(s_le, L + 1)
                c.activation(rep[:, :, 0:NE], lgt[:, :, 0:NE], ACT.Exp).then_inc(s_ee, 1)
                phase_end(act, L, 3)

                def group(g, chunks, before):
                    first_n, first_y = (L * CHUNKS + g * NCH) * NBLK, (L * (NG + 1) + g) * NBLK

                    def copy_out(blk):
                        Y = first_y + blk
                        act.wait_ge(s_yt, Y * 2 + 1)
                        for f in range(KD):
                            if f == 0:
                                act.wait_ge(s_y0, Y + 1)
                            else:
                                act.wait_ge(s_m2, first_n + blk * chunks + chunks + 3)
                            c.activation(ysb[:, f], ps[:, 5 + f, :], ACT.Copy).then_inc(s_ye, 1)

                    def blk_body(blk, lagged, age_of):
                        for k in range(chunks):
                            Q = first_n + blk * chunks + k
                            act.wait_ge(s_h, Q + 1)
                            act.wait_ge(s_lo, Q + 4 - slot_age(k, age_of, 3))
                            apart(act)
                            c.activation(hbuf[:, k % 3, :], ps[:, k % 3, :], ACT.Relu,
                                         bias=b1[:, ds(g * NCH + k, 1)]).then_inc(s_r, 1)
                            if lagged and k == 1:
                                copy_out(blk - 1)
                    blk_body(0, before, before or NCH)
                    with act.Fori(1, NBLK) as blk:
                        blk_body(blk, True, chunks)

                group(0, NCH, 0)
                with act.Fori(1, NG) as g:
                    group(g, NCH, NCH)
                group(NG, NCS, NCH)
                act.wait_ge(s_m2, (L + 1) * CHUNKS * NBLK + 3)
                Y = (L + 1) * (NG + 1) * NBLK
                act.wait_ge(s_yt, Y * 2 - 1)
                for f in range(KD):
                    c.activation(ysb[:, f], ps[:, 5 + f, :], ACT.Copy).then_inc(s_ye, 1)
                phase_end(act, L, 4)

        @block.gpsimd
        def _(pool):
            p = nc.gpsimd
            pool.sem_inc(s_pl, 4)
            pool.sem_inc(s_wl, 11)
            pool.sem_inc(s_lo, 3)
            for r in range(2):
                pool.sem_inc(s_pd[r], 64)
                pool.sem_inc(s_vd[r], 64)
            with pool.Fori(0, NL) as L:
                def qk_lo(b, r):
                    for m in range(2):
                        for f in range(2):
                            pool.wait_ge(s_ph, (L * NBLK + b * 2 + r) * 4 + m * 2 + f + 1)
                            p.tensor_tensor(qkst[:, r, m, 1, f], fqk[:, m, f], qkst[:, r, m, 0, f].bitcast(F32),
                                            ALU.subtract).then_inc(s_pl, 1)

                with pool.Fori(0, B - 1) as b:
                    for r in range(2):
                        qk_lo(b, r)
                pool.wait_ge(s_pj, (L * NBLK + 4) * 6)
                pool.wait_ge(s_pl, (L * NBLK + 6) * 4 + 4)
                apart(pool)
                p.memset(stack32[64:P, 0, 1], 0.0).then_inc(s_zero[0], 1)
                pool.wait_ge(s_zero[0], L + 1)
                for r in range(2):
                    qk_lo(B - 1, r)
                phase_end(pool, L, 0)
                for r in (1, 2):
                    if r == 2:
                        for s in range(2):
                            pool.wait_ge(s_pd[s], (L * B + B) * 64 + 64)
                        apart(pool)
                    for o in range(2):
                        p.memset(stack32[64:P, r, o], 0.0).then_inc(s_zero[r], 1)
                pool.wait_ge(s_bo, L * 32 + 16)
                pool.wait_ge(s_zero[2], (L + 1) * 2)
                apart(pool)
                with pool.Fori(0, NT) as t:
                    xt = x[:, ds(t * D, D)]
                    p.tensor_tensor(xt, xt, bo, ALU.add).then_inc(s_bod, 1)
                for n in (1, 2, 3):
                    phase_end(pool, L, n)

                def weights_lo(g, c):
                    pool.wait_ge(s_wh, L * CHUNKS + g * NCH + c + 1)
                    p.tensor_tensor(w1s[:, c, :, 1, :], raw[:, c % 8, 0:256].rearrange("p (k n) -> p k n", k=KD),
                                    w1s[:, c, :, 0, :].bitcast(F32), ALU.subtract)
                    p.tensor_tensor(w2s[:, c, 1, :], raw[:, c % 8, 256:512], w2s[:, c, 0, :].bitcast(F32),
                                    ALU.subtract).then_inc(s_wl, 1)

                def group(g, chunks, head, following):
                    first_n = (L * CHUNKS + g * NCH) * NBLK

                    def blk_body(blk, first=False, last=False):
                        for c in range(chunks):
                            if first and head + c < chunks:
                                weights_lo(g, head + c)
                            pool.wait_ge(s_hi, first_n + blk * chunks + c + 1)
                            p.tensor_tensor(hsp[:, c % 3, 1, :], hbuf[:, c % 3, :], hsp[:, c % 3, 0, :].bitcast(F32),
                                            ALU.subtract).then_inc(s_lo, 1)
                            if last and 0 <= c - 3 < min(WHEAD, following):
                                weights_lo(g + 1, c - 3)
                    blk_body(0, first=True)
                    with pool.Fori(1, NBLK - 1) as blk:
                        blk_body(blk)
                    blk_body(NBLK - 1, last=True)

                for c in range(FIRST_WHEAD):
                    weights_lo(0, c)
                group(0, NCH, FIRST_WHEAD, NCH)
                with pool.Fori(1, NG - 1) as g:
                    group(g, NCH, WHEAD, NCH)
                group(NG - 1, NCH, WHEAD, NCS)
                group(NG, NCS, WHEAD, 0)
                phase_end(pool, L, 4)

        @block.tensor
        def _(pe):
            mm, tr = nc.tensor.matmul, nc.tensor.transpose
            pe.sem_inc(s_tp, 2)
            pe.sem_inc(s_vt, 2)
            pe.sem_inc(s_pv, 2)
            pe.sem_inc(s_mtp, 2)
            pe.sem_inc(s_mo, 2)
            pe.sem_inc(s_lgt, 2)
            pe.sem_inc(s_m2, 3)
            pe.sem_inc(s_yt, 1)
            pe.wait_ge(s_const, 48)
            with pe.Fori(0, NL) as L:
                def transpose_x(k, blk, r):
                    pe.wait_ge(s_xn, k * NBLK + blk + 1)
                    pe.wait_ge(s_xl, k * NBLK + blk + 1)
                    for f in range(KD):
                        for j in range(TPB):
                            last = tr(ps[:, 2 + 2 * r + f, j * P:j * P + P], xn[:, r, j, f * P:f * P + P], ident[:, :])
                    last.then_inc(s_tp, 1)

                def qkv_block(b, r, ahead):
                    blk = b * 2 + r
                    n = L * NBLK + blk
                    pe.wait_ge(s_xl, L * 2 * NBLK + blk + 3)
                    for m in range(3):
                        for f in range(2):
                            j = m * 2 + f
                            pe.wait_ge(s_pf, n * 6 + j + 1)
                            for e, (ws, xs) in enumerate(PRODUCTS):
                                for k in range(KD):
                                    last = mm(ps[:, j % 2, :], wqkv[:, m, k, ws, f * P:f * P + P],
                                              x_part(blk, k, xs), start=e == 0 and k == 0,
                                              stop=e == 2 and k == KD - 1)
                            last.then_inc(s_pj, 1)
                    if ahead:
                        transpose_x(L * 2, blk + 2, r)
                    pe.wait_ge(s_pf, n * 6 + 6 + 2)
                    pe.wait_ge(s_vs, n + 1)
                    for f in range(2):
                        for j in range(TPB):
                            last = tr(ps[:, 6 + f, j * P:j * P + P], vf[:, r, f, j * P:j * P + P], ident[:, :])
                    last.then_inc(s_vt, 1)

                transpose_x(L * 2, 0, 0)
                transpose_x(L * 2, 1, 1)
                pe.wait_ge(s_wsplit, L + 1)
                apart(pe)
                with pe.Fori(0, B - 1) as b:
                    for r in range(2):
                        qkv_block(b, r, True)
                for r in range(2):
                    qkv_block(B - 1, r, False)
                phase_end(pe, L, 0)

                def base(u):
                    return L * LAYER_JOBS + NJ + 1 + u * STEP_JOBS

                def max_job(task, ring, r, j):
                    i, first, w, heads = MAX_JOBS[j]
                    bank = ps[:, JOB_BANKS[ring % 3], 0:w * len(heads)].rearrange("p (h k) -> p h k", k=w)
                    diagonal = first + w == (i + 1) * P
                    pe.wait_ge(s_mr, task + 1)
                    for e, h in enumerate(heads):
                        last = mm(bank[:, e, :], stack[:, r, 0, h, i * P:i * P + P],
                                  stack[:, r, 1, h, first:first + w], start=e == 0,
                                  stop=not diagonal and e == len(heads) - 1, skip_group_check=True)
                    if diagonal:
                        last = mm(bank[:, :, w - P:w], identb[:, :],
                                  maskq[:, :].unsqueeze(1).broadcast_to([P, len(heads), P]),
                                  start=False, stop=True, skip_group_check=True)
                    last.then_inc(s_mj, 1)

                def scores(U, r, s, half):
                    qt, kb, w = SLOTS[s]
                    pe.wait_ge(s_pe, (U * NS + s) * 2 + half + 1)
                    for e in range(2):
                        h = 2 * half + e
                        last = mm(ps[:, h, BLK - w:], stack[:, r, 1, h, kb * P:kb * P + P],
                                  stack[:, r, 0, h, (qt + 1) * BLK - w:(qt + 1) * BLK],
                                  start=True, stop=kb < 4 * qt, skip_group_check=True)
                        if kb >= 4 * qt:
                            last = mm(ps[:, h, BLK - w:BLK - w + P], identb[:, :], maskk[:, :], start=False, stop=True,
                                      skip_group_check=True)
                    last.then_inc(s_st, 1)

                def values(U, turn, r, s):
                    qt, kb, w = SLOTS[s]
                    if kb == 0:
                        pe.wait_ge(s_ov, U * 2 + qt + 1)
                    if s == 0:
                        pe.wait_ge(s_vl[r], stack_count(L, turn, r) // 7)
                    pe.wait_ge(s_pe, (U * NS + s) * 2 + 2 + 2)
                    for h in range(HG):
                        last = mm(ps[32 * h:32 * h + 32, 6, BLK - w:], vreg[:, r, kb, h, :],
                                  pexp[:, (s % 2) * 2 + h // 2, h % 2, BLK - w:], start=kb == 0,
                                  stop=kb == 4 * qt + 3, skip_group_check=True)
                    last.then_inc(s_pv, 1)

                def transpose_out(U, qt, task, ring):
                    pe.wait_ge(s_ov, U * 2 + qt + 1 + 1)
                    pe.wait_ge(s_mr, task + 1)
                    for j in range(4):
                        last = tr(ps[:, JOB_BANKS[ring % 3], j * P:j * P + P], osb[:, j * P:j * P + P], ident[:, :])
                    last.then_inc(s_mj, 1)

                def transpose_max(U, task, ring):
                    pe.wait_ge(s_neg, U + 1)
                    pe.wait_ge(s_mr, task + 1)
                    apart(pe)
                    tr(ps[0:32, JOB_BANKS[ring % 3], 0:P], mneg, ident[:, :]).then_inc(s_mj, 1)

                def first_scores(U, r):
                    pe.wait_ge(s_mrow, (U + 1) * 32)
                    for half in range(2):
                        scores(U, r, 0, half)

                def step(turn, r, ahead=True):
                    u = turn * 3 + r
                    U = L * NU + u
                    ring = r * STEP_JOBS
                    job = 0
                    if ahead:
                        pe.wait_ge(s_stk[(r + 1) % 3], stack_count(L, turn + (r + 1) // 3, (r + 1) % 3))
                    for s in range(NS):
                        until = min(NJ, NJ * (s + 1) // MAX_SLOTS) if ahead else 0

                        def next_job(job):
                            if job < until:
                                max_job(base(u) + task_of(job), ring + task_of(job), (r + 1) % 3, job)
                                return job + 1
                            return job

                        for half in range(2):
                            if s:
                                scores(U, r, s, half)
                            job = next_job(job)
                        if s:
                            values(U, turn, r, s - 1)
                        while job < until:
                            job = next_job(job)
                        if s == 6:
                            at = OUT0_AT if ahead else 0
                            transpose_out(U, 0, base(u) + at, ring + at)
                        if ahead and s == MAX_SLOTS:
                            transpose_max(U + 1, base(u) + MAX_AT, ring + MAX_AT)
                    values(U, turn, r, NS - 1)
                    if ahead:
                        first_scores(U + 1, (r + 1) % 3)
                    at = OUT1_AT if ahead else 1
                    transpose_out(U, 1, base(u) + at, ring + at)

                pe.wait_ge(s_stk[0], stack_count(L, 0, 0))
                for j in range(NJ):
                    max_job(L * LAYER_JOBS + j, j, 0, j)
                transpose_max(L * NU, L * LAYER_JOBS + NJ, NJ)
                first_scores(L * NU, 0)
                with pe.Fori(0, 5) as i:
                    for r in range(3):
                        step(i, r)
                step(5, 0, ahead=False)
                phase_end(pe, L, 1)

                def merge_transpose(i, r):
                    pe.wait_ge(s_mev, L * NBLK + i * 2 + r + 1)
                    apart(pe)
                    for f in range(KD):
                        for j in range(TPB):
                            last = tr(ps[:, 2 * r + f, j * P:j * P + P],
                                      attn[:, i * KD + f, TPB * r + j, :], ident[:, :])
                    last.then_inc(s_mtp, 1)

                def merge_product(i, r):
                    n = L * NBLK + i * 2 + r
                    pe.wait_ge(s_mev, n + 1 + 2)
                    pe.wait_ge(s_ma, n + 1)
                    for j in range(TPB):
                        for k in range(KD):
                            last = mm(ps[:, 4 + 2 * r + j // 2, (j % 2) * D:(j % 2) * D + D],
                                      mT[:, r, k, j * P:j * P + P], wo[:, k * D:k * D + D],
                                      start=k == 0 and j % 2 == 0, stop=k == KD - 1, skip_group_check=True)
                    last.then_inc(s_mo, 1)

                merge_transpose(0, 0)
                pe.wait_ge(s_bo, (L + 1) * 32)
                apart(pe)
                for i in range(NBLK // 2 - 1):
                    merge_transpose(i, 1)
                    merge_product(i, 0)
                    merge_transpose(i + 1, 0)
                    merge_product(i, 1)
                merge_transpose(NBLK // 2 - 1, 1)
                merge_product(NBLK // 2 - 1, 0)
                merge_product(NBLK // 2 - 1, 1)
                phase_end(pe, L, 2)

                def route_block(i, r, ahead):
                    blk = i * 2 + r
                    n = L * NBLK + blk
                    pe.wait_ge(s_xl, (L * 2 + 1) * NBLK + blk + 3)
                    pe.wait_ge(s_lge, n + 1)
                    for e, (ws, xs) in enumerate(PRODUCTS):
                        for k in range(KD):
                            last = mm(ps[:, r, :], hsp[:, 0, ws, k * P:k * P + P], x_part(blk, k, xs),
                                      start=e == 0 and k == 0, stop=e == 2 and k == KD - 1)
                    last.then_inc(s_lg, 1)
                    if ahead:
                        transpose_x(L * 2 + 1, blk + 2, r)
                    pe.wait_ge(s_lge, n + 1 + 2)
                    pe.wait_ge(s_lgd, n + 1)
                    apart(pe)
                    for j in range(TPB):
                        last = tr(ps[:, 6 + r, j * NE:j * NE + NE], lgT[0:NE, r, j * P:j * P + P],
                                  ident[0:NE, 0:NE])
                    last.then_inc(s_lgt, 1)

                transpose_x(L * 2 + 1, 0, 0)
                transpose_x(L * 2 + 1, 1, 1)
                pe.wait_ge(s_rsp, L + 1)
                apart(pe)
                with pe.Fori(0, NBLK // 2 - 1) as i:
                    for r in range(2):
                        route_block(i, r, True)
                for r in range(2):
                    route_block(NBLK // 2 - 1, r, False)
                pe.wait_ge(s_gs, L + 1)
                for n in range(NBLK):
                    pe.wait_ge(s_gd, L * NBLK + n + 1)
                    for j in range(TPB):
                        last = tr(ps[:, n % 2, 64 * j:64 * j + 64].bitcast(BF16), gst[:, n * TPB + j, :], identb[:, :])
                    last.then_inc(s_gt, 1)
                phase_end(pe, L, 3)

                def group(g, chunks, before, following):
                    first_n, first_y = (L * CHUNKS + g * NCH) * NBLK, (L * (NG + 1) + g) * NBLK
                    first_w = L * CHUNKS + g * NCH

                    def gate_rows(blk, c, odd):
                        Q = first_n + blk * chunks + c
                        pe.wait_ge(s_hg, Q + 1)
                        mm(ps[:, 3 + (odd + c) % 2, :], sel[:, ds((g * NCH + c) * P, P)], gT[:, ds(blk * BLK, BLK)],
                           start=True, stop=True).then_inc(s_g, 1)

                    def hidden(blk, c, age_of):
                        Q = first_n + blk * chunks + c
                        pe.wait_ge(s_r, Q + 4 - slot_age(c, age_of, 3))
                        for e, (ws, xs) in enumerate(PRODUCTS):
                            for k in range(KD):
                                last = mm(ps[:, c % 3, :], w1s[:, c, k, ws, :], x_part(blk, k, xs),
                                          start=e == 0 and k == 0, stop=e == 2 and k == KD - 1)
                        last.then_inc(s_h, 1)

                    def summed(Q, Y, blk, c, of):
                        pe.wait_ge(s_lo, Q + 1 + 3)
                        for f in range(KD):
                            if c == 0:
                                pe.wait_ge(s_ye, Y * KD + f + 1)
                                if of == NCS:
                                    for s in range(3):
                                        mm(ps[:, 5 + f, :], b2s[:, s, f * P:f * P + P], gT[:, ds(blk * BLK, BLK)],
                                           start=s == 0, stop=False)
                            for e, (ws, xs) in enumerate(PRODUCTS):
                                last = mm(ps[:, 5 + f, :], w2s[:, c, ws, f * P:f * P + P], hsp[:, c % 3, xs, :],
                                          start=c == 0 and e == 0 and of != NCS, stop=c == of - 1 and e == 2)
                            if c == of - 1 and f == 0:
                                last.then_inc(s_y0, 1)
                        last.then_inc(s_m2, 1)

                    def transpose_out(blk, f):
                        Y = first_y + blk
                        pe.wait_ge(s_ye, (Y + 1) * KD + KD)
                        pe.wait_ge(s_ya, Y * 2 + f + 1)
                        for j in range(2):
                            for k in range(KD):
                                last = tr(ps[:, 7, (j * KD + k) * P:(j * KD + k) * P + P],
                                          ysb[:, k, (2 * f + j) * P:(2 * f + j) * P + P], ident[:, :])
                        last.then_inc(s_yt, 1)

                    def blk_body(blk, odd, lagged=True, first=False):
                        of = before if first else chunks
                        for c in range(chunks):
                            n = first_n + blk * chunks + c
                            gate_rows(blk, c, odd)
                            if first:
                                pe.wait_ge(s_wl, first_w + c + 1 + 11)
                            hidden(blk, c, of or NCH)
                            if lagged and c == 2 and chunks == NCS:
                                transpose_out(blk - 1, 0)
                            if c >= 2:
                                summed(n - 2, first_y + blk, blk, c - 2, chunks)
                            elif lagged:
                                summed(n - 2, first_y + blk - 1, NBLK - 1 if first else blk - 1, of - 2 + c, of)
                            if lagged and c == 2 and chunks != NCS:
                                transpose_out(blk - 1, 0)
                            if lagged and c == min(chunks - 1, 4):
                                transpose_out(blk - 1, 1)
                    blk_body(0, 0, lagged=before, first=True)
                    with pe.Fori(0, NBLK // 2 - 1) as i:
                        for odd in (1, 0):
                            blk_body(i * 2 + 2 - odd, odd)
                    blk_body(NBLK - 1, 1)
                    if not following:
                        last_n = first_n + NBLK * chunks
                        for c in (chunks - 2, chunks - 1):
                            summed(last_n - chunks + c, first_y + NBLK - 1, NBLK - 1, c, chunks)
                        for f in range(2):
                            transpose_out(NBLK - 1, f)

                group(0, NCH, 0, NCH)
                with pe.Fori(1, NG) as g:
                    group(g, NCH, NCH, NCH)
                group(NG, NCS, NCH, 0)
                phase_end(pe, L, 4)


_SHAPES = dict(
    x=(B, T, D), wqkv=(NL, 3, D, D), bqkv=(NL, P, 6), wo=(NL, D, D), bo=(NL, D),
    rw=(D, P), rb=(P, 1), w1=(D, HIDS), w2=(HIDS, D), b1=(P, CHUNKS), b2=(NE + 32, D),
    rows=(NL, 2, SROWS - 48, T), ident=(P, P), masks=(2, P, P), sel=(P, HIDS))


def arrays(i):
    f = np.float32
    i = {k: np.asarray(v) for k, v in i.items()}
    A, Bp, F = "L0_attn_a_", "L0_attn_b_", "L0_ffn_"
    r = {"x": i[A + "x"]}
    r["wqkv"] = np.stack([np.stack([i[A + "k_w"].T, i[A + "q_w"].T, i[A + "v_w"].T]),
                          np.stack([i[Bp + "Wq"], i[Bp + "Wk"], i[Bp + "Wv"]])])
    bias = np.stack([np.stack([i[A + "k_b"], i[A + "q_b"], i[A + "v_b"]]),
                     np.stack([i[Bp + "bq"], i[Bp + "bk"], i[Bp + "bv"]])])
    r["bqkv"] = bias.reshape(NL, 6, P).transpose(0, 2, 1)
    r["wo"] = np.stack([i[A + "o_w"].T, i[Bp + "Wo"]])
    r["bo"] = np.stack([i[A + "o_b"], i[Bp + "bo"]])
    rw = np.zeros((D, P), f)
    rw[:, :NE] = i[F + "router_w"]
    r["rw"] = rw
    rb = np.zeros((P, 1), f)
    rb[:NE, 0] = i[F + "router_b"]
    r["rb"] = rb
    w1 = np.zeros((D, HIDS), f)
    w2 = np.zeros((HIDS, D), f)
    b1 = np.zeros((HIDS,), f)
    n, m = NE * HID, (NE + NSH) * HID
    w1[:, :n] = i[F + "rw1"].transpose(1, 0, 2).reshape(D, n)
    w1[:, n:m] = i[F + "sw1"].transpose(1, 0, 2).reshape(D, m - n)
    w2[:n] = i[F + "rw2"].reshape(n, D)
    w2[n:m] = i[F + "sw2"].reshape(m - n, D)
    b1[:n] = i[F + "rb1"].reshape(n)
    b1[n:m] = i[F + "sb1"].reshape(m - n)
    r["w1"], r["w2"], r["b1"] = w1, w2, b1.reshape(CHUNKS, P).T
    b2 = np.zeros((NE + 32, D), f)
    b2[:NE] = i[F + "rb2"]
    b2[NE:NE + NSH] = i[F + "sb2"]
    r["b2"] = b2
    t = np.arange(T, dtype=f)
    rows = np.zeros((NL, 2, SROWS - 48, T), f)
    rows[0, 0, 16], rows[0, 0, 17] = -t, 1.0
    rows[0, 1, 16], rows[0, 1, 17] = 1.0, t
    rows[:, 1, 18:20] = 1.0
    r["rows"] = rows
    r["ident"] = np.eye(P, dtype=f)
    q, k = np.arange(P)[:, None], np.arange(P)[None, :]
    r["masks"] = np.stack([np.where(k > q, NEG, 0.0), np.where(q > k, NEG, 0.0)]).astype(f)
    sel = np.zeros((P, HIDS), np.float16)
    for e in range(NE + NSH):
        for row in ((e, NE + e, 2 * NE + e) if e < NE else (3 * NE + e - NE,)):
            sel[row, e * HID:(e + 1) * HID] = 1.0
    r["sel"] = sel
    return {k: np.ascontiguousarray(v) for k, v in r.items()}


def kernel(**inputs):
    import concourse.bacc as _bacc
    from concourse.bass_utils import run_bass_kernel_spmd as _run

    nc = _bacc.Bacc("TRN2", target_bir_lowering=False, num_devices=1)
    laid = arrays(inputs)
    aps = {k: nc.dram_tensor(f"in_{k}", shape, F16 if k == "sel" else F32, kind="ExternalInput").ap()
           for k, shape in _SHAPES.items()}
    out = nc.dram_tensor("out_0", (B, T, D), F32, kind="ExternalOutput").ap()
    build(nc, aps, out)
    r = _run(nc, [{f"in_{k}": laid[k] for k in _SHAPES}], core_ids=[0])
    return r.results[0]["out_0"]
```
